# Optimizing a Trainium2 kernel written in Bass

```python
import numpy as np
import jax
import jax.numpy as jnp

def _softmax(x, axis=-1):
    return jax.nn.softmax(x, axis=axis)

def _gelu(x):
    return jax.nn.gelu(x, approximate=True)

def _silu(x):
    return jax.nn.silu(x)

def _sigmoid(x):
    return jax.nn.sigmoid(x)

def _layernorm(x, axis=-1, eps=1e-05):
    m = jnp.mean(x, axis=axis, keepdims=True)
    v = jnp.var(x, axis=axis, keepdims=True)
    return (x - m) / jnp.sqrt(v + eps)

def _scatter_add(tgt, idx, src, axis=0):
    return tgt.at[idx].add(src)

def _segment_sum(src, seg, n):
    return jax.ops.segment_sum(src, seg, n)
kernel_name = 'mk_recurrent_d1_jaxref_r4_a6d66e'

def setup_inputs(seed: int=0):
    np.random.seed(seed)
    _w = jnp.asarray

    def _L0_attn_setup():
        import jax, jax.numpy as jnp
        import numpy as np
        THETA = 10000.0

        def _rope_tables(seq_len, dk, dtype):
            pos = jnp.arange(seq_len, dtype=jnp.float32)[:, None]
            k = jnp.arange(dk // 2, dtype=jnp.float32)[None, :]
            angle = pos / THETA ** (2.0 * k / dk)
            return (jnp.sin(angle).astype(dtype), jnp.cos(angle).astype(dtype))

        def _apply_rope(t, sin, cos):
            even = t[..., 0::2]
            odd = t[..., 1::2]
            even_out = even * cos - odd * sin
            odd_out = even * sin + odd * cos
            out = jnp.stack([even_out, odd_out], axis=-1)
            return out.reshape(t.shape)
        key = jax.random.key(seed)
        ks = jax.random.split(key, 5)
        b, s, d = (2, 512, 256)
        std = np.sqrt(2.0 / (d + d))
        return {'x': jax.random.normal(ks[0], (b, s, d), dtype=jnp.float32), 'wq': jax.random.normal(ks[1], (d, d), dtype=jnp.float32) * std, 'wk': jax.random.normal(ks[2], (d, d), dtype=jnp.float32) * std, 'wv': jax.random.normal(ks[3], (d, d), dtype=jnp.float32) * std, 'wo': jax.random.normal(ks[4], (d, d), dtype=jnp.float32) * std}
    _L0_attn_in = _L0_attn_setup()

    def _L0_ffn_setup():
        import jax, jax.numpy as jnp
        import numpy as np
        DIM = 256
        HIDDEN = 768
        SCALE = 1.0 / 127.0

        def _dequant(w_int, dtype):
            return w_int.astype(dtype) * jnp.asarray(SCALE, dtype)
        key = jax.random.key(seed)
        k_x, k_g, k_u, k_d = jax.random.split(key, 4)
        x = jax.random.normal(k_x, (4, 512, DIM), dtype=jnp.float32)
        w_gate = jax.random.randint(k_g, (HIDDEN, DIM), -127, 128, dtype=jnp.int32)
        w_up = jax.random.randint(k_u, (HIDDEN, DIM), -127, 128, dtype=jnp.int32)
        w_down = jax.random.randint(k_d, (DIM, HIDDEN), -127, 128, dtype=jnp.int32)
        return {'x': x, 'w_gate': w_gate, 'w_up': w_up, 'w_down': w_down}
    _L0_ffn_in = _L0_ffn_setup()
    _d = {'L0_attn_x': _L0_attn_in['x'], 'L0_attn_wq': _L0_attn_in['wq'], 'L0_attn_wk': _L0_attn_in['wk'], 'L0_attn_wv': _L0_attn_in['wv'], 'L0_attn_wo': _L0_attn_in['wo'], 'L0_ffn_w_gate': _L0_ffn_in['w_gate'], 'L0_ffn_w_up': _L0_ffn_in['w_up'], 'L0_ffn_w_down': _L0_ffn_in['w_down']}
    _x0 = _d['L0_attn_x']
    _d['L0_attn_x'] = jax.random.normal(jax.random.fold_in(jax.random.key(seed), 1), (8, 1024, 256), dtype=_x0.dtype)
    del _x0
    return _d

def reference(L0_attn_x, L0_attn_wq, L0_attn_wk, L0_attn_wv, L0_attn_wo, L0_ffn_w_gate, L0_ffn_w_up, L0_ffn_w_down):

    def _L0_attn_ref(x, wq, wk, wv, wo):
        import jax, jax.numpy as jnp
        import numpy as np
        THETA = 10000.0

        def _rope_tables(seq_len, dk, dtype):
            pos = jnp.arange(seq_len, dtype=jnp.float32)[:, None]
            k = jnp.arange(dk // 2, dtype=jnp.float32)[None, :]
            angle = pos / THETA ** (2.0 * k / dk)
            return (jnp.sin(angle).astype(dtype), jnp.cos(angle).astype(dtype))

        def _apply_rope(t, sin, cos):
            even = t[..., 0::2]
            odd = t[..., 1::2]
            even_out = even * cos - odd * sin
            odd_out = even * sin + odd * cos
            out = jnp.stack([even_out, odd_out], axis=-1)
            return out.reshape(t.shape)
        b, s, d = x.shape
        h = 16
        dk = d // h
        Q = jnp.einsum('bsd,ed->bse', x, wq).reshape(b, s, h, dk).transpose(0, 2, 1, 3)
        K = jnp.einsum('bsd,ed->bse', x, wk).reshape(b, s, h, dk).transpose(0, 2, 1, 3)
        V = jnp.einsum('bsd,ed->bse', x, wv).reshape(b, s, h, dk).transpose(0, 2, 1, 3)
        sin, cos = _rope_tables(s, dk, x.dtype)
        Q = _apply_rope(Q, sin, cos)
        K = _apply_rope(K, sin, cos)
        scale = 1.0 / np.sqrt(dk)
        scores = jnp.einsum('bhqd,bhkd->bhqk', Q, K) * scale
        causal = jnp.tril(jnp.ones((s, s), dtype=bool))
        scores = jnp.where(causal, scores, -jnp.inf)
        probs = jax.nn.softmax(scores, axis=-1)
        attn = jnp.einsum('bhqk,bhkd->bhqd', probs, V)
        attn = attn.transpose(0, 2, 1, 3).reshape(b, s, d)
        return jnp.einsum('bse,de->bsd', attn, wo)

    def _L0_ffn_ref(x, w_gate, w_up, w_down):
        import jax, jax.numpy as jnp
        import numpy as np
        DIM = 256
        HIDDEN = 768
        SCALE = 1.0 / 127.0

        def _dequant(w_int, dtype):
            return w_int.astype(dtype) * jnp.asarray(SCALE, dtype)
        wg = _dequant(w_gate, x.dtype)
        wu = _dequant(w_up, x.dtype)
        wd = _dequant(w_down, x.dtype)
        gate = jnp.einsum('bsd,hd->bsh', x, wg)
        up = jnp.einsum('bsd,hd->bsh', x, wu)
        h = jax.nn.silu(gate) * up
        return jnp.einsum('bsh,dh->bsd', h, wd)
    x = L0_attn_x
    xn = _layernorm(x, axis=-1)
    s = _L0_attn_ref(xn, L0_attn_wq, L0_attn_wk, L0_attn_wv, L0_attn_wo)
    g = _silu(_L0_ffn_ref(xn, L0_ffn_w_gate, L0_ffn_w_up, L0_ffn_w_down))
    x = x + s * g
    return x

_drawn_inputs = setup_inputs


def setup_inputs(seed=0):
    import zlib

    import numpy as np

    out = dict(_drawn_inputs(seed))
    spreads = {}
    factors = {}
    for name, (base, spread) in spreads.items():
        noise = np.random.default_rng([zlib.crc32(name.encode()), seed]).standard_normal(out[name].shape)
        drawn = base * np.exp(spread * noise) if base else spread * noise
        out[name] = jnp.asarray(drawn.astype(out[name].dtype))
    for name, factor in factors.items():
        out[name] = (out[name] * factor).astype(out[name].dtype)
    return out
```

```python
import concourse.bass as bass
from concourse import mybir
from contextlib import ExitStack

F32 = mybir.dt.float32
F16 = mybir.dt.float16
BF16 = mybir.dt.bfloat16
I32 = mybir.dt.int32
ACT = mybir.ActivationFunctionType
ALU = mybir.AluOpType
AX = mybir.AxisListType

P = 128
B, S, D = 8, 1024, 256
H, DK = 16, 16
HID = 768
EPS = 1e-5
QSCALE = 1.0 / 127.0
HSCALE = 0.125
KD = D // P
MH = HID // P
CH = 512
CT = CH // P
HALVES = S // CH
PAIRS = DK // 2
GH = 4
NG = H // GH
QB = S // P
VW = 32
PARTS = 3
STACK = 6 * DK
MASKED = -3.0e38
Q_BANDS = (0, 1, 2, 0, 1, 0)
K_BANDS = (0, 0, 0, 1, 1, 2)


class Stage:

    def __init__(self, ctx, nc, name, k, per):
        self.sem = ctx.enter_context(nc.semaphore(name))
        self.k, self.per = k, per
        self.lead = per + 2

    def start(self, eng):
        eng.sem_inc(self.sem, self.lead * self.k)

    def after(self, step, count=None):
        loop, off = step
        count = self.k if count is None else count
        return loop * (self.per * self.k) + ((off + self.lead) * self.k + count)


def wait(eng, stage, step, count=None):
    eng.wait_ge(stage.sem, stage.after(step, count))


def hold(eng, sem):
    eng.sem_inc(sem, 1)


def earlier(step, n):
    return step[0], step[1] - n


class Chain:

    def __init__(self, eng, sem):
        self.eng, self.sem, self.n = eng, sem, 0

    def __call__(self, instruction):
        instruction.then_inc(self.sem, 1)
        self.n += 1
        self.eng.wait_ge(self.sem, self.n)


def project_phase(nc, ps, keep, x, wq, wk, wv, wo, w_gate, w_up, w_down, cs, scratch):
    q_parts_d, k_parts_d, v_d, gate_d = scratch
    ident, woT = keep["ident"], keep["woT"]
    ctx = ExitStack()
    with ctx:
        sb = lambda n, s, d: ctx.enter_context(nc.sbuf_tensor(n, s, d))
        sem = lambda n: ctx.enter_context(nc.semaphore(n))
        stage = lambda n, k: Stage(ctx, nc, n, k, HALVES)

        wqkT = sb("wqkT", [P, KD, 4, P], F32)
        wvT = sb("wvT", [P, KD, D], F32)
        wguT = sb("wguT", [P, 2, KD, HID], F16)
        wdT = sb("wdT", [P, MH, D], F16)
        trig = sb("trig", [P, 2, 2, S], F32)
        negh = sb("negh", [P, CT], F32)

        xs = sb("xs", [P, 2, CT, D], F32)
        st = sb("st", [P, CT, 6], F32)
        mv = sb("mv", [P, CT, 2], F32)
        ve = sb("ve", [P, CT], F32)
        rstd = sb("rstd", [P, CT], F32)
        xn = sb("xn", [P, CT, D], F32)
        xT = sb("xT", [P, KD, CH], F32)
        xTh = sb("xTh", [P, KD, CH], F16)
        xTl = sb("xTl", [P, KD, CH], F16)
        gs = sb("gs", [P, 2, CT, D], F32)
        vs = sb("vs", [P, CT, H, VW], F32)

        s_const = sem("s_const")
        s_one = sem("s_one")
        s_held = sem("s_held")
        s_wload = sem("s_wload")
        s_prep = sem("s_prep")
        s_wt = sem("s_wt")
        s_we = sem("s_we")
        x_ld = [stage(f"x_ld{i}", 0) for i in range(2)]
        ln_stat, ln_aggr = stage("ln_stat", 1), stage("ln_aggr", 1)
        ln_ve, ln_rs, ln_xn = stage("ln_ve", 1), stage("ln_rs", 1), stage("ln_xn", 1)
        t_pe, t_act, t_lo = stage("t_pe", 1), stage("t_act", 2), stage("t_lo", 1)
        q_pe, k_pe, v_pe = stage("q_pe", 1), stage("k_pe", 1), stage("v_pe", 1)
        rot_mul, rot_add = stage("rot_mul", 2), stage("rot_add", 2)
        part1, rest1, part2, part3 = stage("part1", 2), stage("rest1", 2), stage("part2", 2), stage("part3", 2)
        v_act = stage("v_act", 1)
        gu_pe, silu, hid = stage("gu_pe", MH), stage("silu", MH), stage("hid", MH)
        hid_hi, hid_lo = stage("hid_hi", MH), stage("hid_lo", MH)
        down_pe, gate_act = stage("down_pe", 2), stage("gate_act", 2)
        qk_st, v_st, g_st = stage("qk_st", 32), stage("v_st", 16), stage("g_st", 16)

        T0, Q0, K0, V0 = 0, 2, 4, 6
        loads = 16 * 11

        with ExitStack() as pre, nc.Block() as block:
            raw = pre.enter_context(nc.sbuf_tensor("raw", [P, 8, D], F32))
            rawi = pre.enter_context(nc.sbuf_tensor("rawi", [P, 18, D], I32))
            rawf = pre.enter_context(nc.sbuf_tensor("rawf", [P, 18, D], F32))

            @block.sync
            def _(sp):
                for i, w in enumerate((wq, wk)):
                    rows = w.rearrange("(h i two) d -> two i h d", i=PAIRS, two=2)
                    for eo in range(2):
                        for i8 in range(PAIRS):
                            sp.dma_start(raw[H * i8:H * (i8 + 1), 2 * i + eo, :], rows[eo, i8]).then_inc(s_wload, 16)
                for i, w in enumerate((wv, wo)):
                    sp.dma_start(raw[:, 4 + 2 * i:6 + 2 * i, :], w.rearrange("(m p) d -> p m d", p=P)).then_inc(s_wload, 16)
                for i, w in enumerate((w_gate, w_up, w_down.rearrange("d (m e) -> (d m) e", m=3))):
                    if i < 2:
                        src = w.rearrange("(m p) d -> p m d", p=P)
                    else:
                        src = None
                    if src is not None:
                        sp.dma_start(rawi[:, 6 * i:6 * i + 6, :], src).then_inc(s_wload, 16)
                sp.dma_start(rawi[:, 12:18, :].rearrange("p (a m) e -> p a (m e)", a=2),
                             w_down.rearrange("(a p) e -> p a e", p=P)).then_inc(s_wload, 16)
                sp.dma_start(trig[:, :, :, :], cs[:, :, :, :]).then_inc(s_const, 16)
                sp.wait_ge(s_const, 16)

            n_w = 16 * (4 * PAIRS + 5)

            @block.gpsimd
            def _(pool):
                ch = Chain(pool, s_prep)
                ch(pool.memset(ident[:, :], 0.0))
                ch(pool.affine_select(out=ident[:, :], in_=ident[:, :], compare_op=ALU.not_equal, fill=1.0,
                                      base=0, pattern=[[-1, P]], channel_multiplier=1))
                ch(pool.memset(negh[:, :], -0.5))
                ch(pool.memset(vs[:, :, :, :], 0.0))
                ch(pool.memset(vs[:, :, :, DK:DK + 1], 1.0))

            blocks = []
            for kd in range(KD):
                for m in range(4):
                    blocks.append((raw[:, m, kd * P:(kd + 1) * P], wqkT[:, kd, m, :]))
            for m in range(2):
                for kd in range(KD):
                    blocks.append((raw[:, 4 + m, kd * P:(kd + 1) * P], wvT[:, kd, m * P:(m + 1) * P]))
            for m in range(2):
                for kd in range(KD):
                    blocks.append((raw[:, 6 + m, kd * P:(kd + 1) * P], woT[:, kd, m * P:(m + 1) * P]))
            for gu in range(2):
                for kd in range(KD):
                    for m in range(MH):
                        blocks.append((rawf[:, 6 * gu + m, kd * P:(kd + 1) * P],
                                       wguT[:, gu, kd, m * P:(m + 1) * P]))
            down = rawf[:, 12:18, :].rearrange("p (a m) e -> p a (m e)", a=2)
            for m in range(MH):
                for a in range(2):
                    blocks.append((down[:, a, m * P:(m + 1) * P], wdT[:, m, a * P:(a + 1) * P]))

            @block.vector
            def _(dve):
                dve.wait_ge(s_wload, n_w)
                dve.tensor_copy(rawf[:, :, :], rawi[:, :, :]).then_inc(s_one, 1)
                for n, (_, dst) in enumerate(blocks):
                    dve.wait_ge(s_wt, n + 1)
                    dve.tensor_copy(dst, ps[:, n % 8, 0:P]).then_inc(s_we, 1)

            @block.tensor
            def _(pe):
                pe.wait_ge(s_prep, 2)
                pe.wait_ge(s_wload, n_w)
                pe.wait_ge(s_one, 1)
                for n, (src, _) in enumerate(blocks):
                    if n >= 8:
                        pe.wait_ge(s_we, n - 7)
                    pe.transpose(ps[:, n % 8, 0:P], src, ident[:, :]).then_inc(s_wt, 1)

        tq = [sb(f"rot{i}", [P, 2, 2, CH], F32) for i in range(2)]
        rr = [sb(f"rr{i}", [P, 2, CH], F32) for i in range(2)]
        r1 = [sb(f"r1{i}", [P, 2, CH], F32) for i in range(2)]
        parts = [[sb(f"parts{i}{j}", [P, PARTS, 2, CH], BF16) for j in range(2)] for i in range(2)]
        sg = sb("sg", [P, 2, CH], F32)
        h32 = sb("h32", [P, 2, CH], F32)
        hh = sb("hh", [P, MH, CH], F16)
        hl = sb("hl", [P, MH, CH], F16)

        x_v = x.rearrange("b (c a p) d -> b c p a d", c=HALVES, p=P)
        qk_dst = [d.rearrange("b (r p) s -> b p r s", p=P) for d in (q_parts_d, k_parts_d)]
        gate_v = gate_d.rearrange("b (c a p) d -> b c p a d", c=HALVES, p=P)
        v_v = v_d.rearrange("b (c a) p e -> b c p a e", c=HALVES)

        with nc.Block() as block:

            def over_batches(eng, chunk):
                with eng.Fori(0, B - 1) as b:
                    for c in range(HALVES):
                        chunk((b, c), True)
                for c in range(HALVES):
                    chunk((B - 1, c), c + 1 < HALVES)

            @block.sync
            def _(sp):
                for s in (qk_st, v_st, g_st):
                    s.start(sp)
                for c in range(HALVES):
                    sp.dma_start(xs[:, c], x_v[0, c]).then_inc(x_ld[c].sem, 16)

                def chunk(step, more):
                    b, c = step
                    if isinstance(b, int):
                        ahead = False
                    else:
                        ahead = True
                    if ahead:
                        wait(sp, ln_xn, step)
                        sp.dma_start(xs[:, c], x_v[b + 1, c]).then_inc(x_ld[c].sem, 16)
                    for i in range(2):
                        wait(sp, part3, step, i + 1)
                        sp.dma_start(qk_dst[i][b, :, :, c * CH:(c + 1) * CH],
                                     parts[i][c].rearrange("p a e s -> p (a e) s")[:, :, :]).then_inc(qk_st.sem, 16)
                    wait(sp, v_act, step)
                    sp.dma_start(v_v[b, c], vs.rearrange("p a h v -> p a (h v)")[:, :, :]).then_inc(v_st.sem, 16)
                    wait(sp, gate_act, step)
                    sp.dma_start(gate_v[b, c], gs[:, c]).then_inc(g_st.sem, 16)

                over_batches(sp, chunk)
                last = (B - 1, HALVES - 1)
                for s in (qk_st, v_st, g_st):
                    wait(sp, s, last)

            def back2(step, m):
                return (step, m - 1) if m >= 2 else (earlier(step, 1), MH + m - 1)

            def x_arrived(eng, step):
                b, c = step
                if c >= HALVES:
                    b, c = b + 1, c - HALVES
                eng.wait_ge(x_ld[c].sem, b * 16 + 16)
                return c

            def nxt(step):
                return step[0], step[1] + 1

            @block.vector
            def _(dve):
                for s in (ln_stat, ln_aggr, ln_xn, t_lo, rot_mul, part3, hid):
                    s.start(dve)

                def stats(step):
                    c = x_arrived(dve, step)
                    wait(dve, ln_aggr, earlier(step, 1))
                    for a in range(CT):
                        ins = dve.bn_stats(st[:, a], xs[:, c, a])
                    ins.then_inc(ln_stat.sem, 1)
                    wait(dve, ln_rs, earlier(step, 1))
                    wait(dve, ln_xn, earlier(step, 1))
                    wait(dve, ln_stat, step)
                    hold(dve, s_held)
                    for a in range(CT):
                        ins = dve.bn_aggr(mv[:, a], st[:, a])
                    ins.then_inc(ln_aggr.sem, 1)

                def normalise(step):
                    c = step[1] % HALVES
                    wait(dve, t_pe, earlier(step, 1))
                    wait(dve, ln_rs, step)
                    for a in range(CT):
                        ins = dve.tensor_scalar(xn[:, a], xs[:, c, a], mv[:, a, 0:1], rstd[:, a:a + 1],
                                                ALU.subtract, ALU.mult)
                    ins.then_inc(ln_xn.sem, 1)

                def low_part(step):
                    wait(dve, t_act, step)
                    dve.tensor_tensor(xTl[:, :, :], ps[:, T0:T0 + 2, :], xTh[:, :, :], ALU.subtract).then_inc(t_lo.sem, 1)

                def rotate(step, i, pe_stage):
                    c = step[1]
                    wait(dve, rot_add, earlier(step, 1), i + 1)
                    wait(dve, pe_stage, step)
                    for t in range(2):
                        ins = dve.tensor_tensor(tq[i][:, t], ps[:, (Q0, K0)[i]:(Q0, K0)[i] + 2, :],
                                                trig[:, t, :, c * CH:(c + 1) * CH], ALU.mult)
                    ins.then_inc(rot_mul.sem, 1)

                def third_part(step, i):
                    wait(dve, part2, step, i + 1)
                    dve.tensor_tensor(parts[i][step[1]][:, 2], r1[i][:, :, :], parts[i][step[1]][:, 1],
                                      ALU.subtract).then_inc(part3.sem, 1)

                def hidden(step, m):
                    wait(dve, hid_hi, *back2(step, m))
                    wait(dve, hid_lo, *back2(step, m))
                    wait(dve, silu, step, m + 1)
                    dve.scalar_tensor_tensor(out=h32[:, m % 2], in0=ps[:, (Q0, K0)[m % 2] + 1, :], scalar=QSCALE * HSCALE,
                                             in1=sg[:, m % 2], op0=ALU.mult, op1=ALU.mult).then_inc(hid.sem, 1)

                stats((0, 0))
                normalise((0, 0))
                low_part((0, 0))

                def chunk(step, more):
                    rotate(step, 0, q_pe)
                    rotate(step, 1, k_pe)
                    if more:
                        stats(nxt(step))
                    hidden(step, 0)
                    if more:
                        normalise(nxt(step))
                    hidden(step, 1)
                    third_part(step, 0)
                    hidden(step, 2)
                    third_part(step, 1)
                    for m in range(3, MH):
                        hidden(step, m)
                    if more:
                        low_part(nxt(step))

                over_batches(dve, chunk)

            @block.gpsimd
            def _(pool):
                for s in (ln_ve, ln_rs, rot_add, rest1, hid_lo):
                    s.start(pool)

                def inverse_root(step):
                    wait(pool, ln_xn, earlier(step, 1))
                    wait(pool, ln_aggr, step)
                    hold(pool, s_held)
                    pool.tensor_scalar(ve[:, :], mv[:, :, 1], EPS, 1.0, ALU.add, ALU.mult).then_inc(ln_ve.sem, 1)
                    wait(pool, ln_ve, step)
                    pool.tensor_tensor(rstd[:, :], ve[:, :], negh[:, :], ALU.pow).then_inc(ln_rs.sem, 1)

                def rotated(step, i):
                    wait(pool, part1, earlier(step, 1), i + 1)
                    wait(pool, rest1, earlier(step, 1), i + 1)
                    wait(pool, rot_mul, step, i + 1)
                    pool.tensor_tensor(rr[i][:, :, :], tq[i][:, :, 0, :], tq[i][:, :, 1, :], ALU.add).then_inc(rot_add.sem, 1)

                def rest(step, i):
                    wait(pool, part2, earlier(step, 1), i + 1)
                    wait(pool, part3, earlier(step, 1), i + 1)
                    wait(pool, rot_add, step, i + 1)
                    wait(pool, part1, step, i + 1)
                    pool.tensor_tensor(r1[i][:, :, :], rr[i][:, :, :], parts[i][step[1]][:, 0], ALU.subtract).then_inc(rest1.sem, 1)

                def low(step, m):
                    if m == 0:
                        wait(pool, down_pe, earlier(step, 1))
                    wait(pool, hid_hi, step, m + 1)
                    pool.tensor_tensor(hl[:, m], h32[:, m % 2], hh[:, m], ALU.subtract).then_inc(hid_lo.sem, 1)

                inverse_root((0, 0))

                def chunk(step, more):
                    rotated(step, 0)
                    rotated(step, 1)
                    if more:
                        inverse_root(nxt(step))
                    rest(step, 0)
                    rest(step, 1)
                    for m in range(MH):
                        low(step, m)

                over_batches(pool, chunk)

            @block.scalar
            def _(act):
                for s in (t_act, part1, part2, v_act, silu, hid_hi, gate_act):
                    s.start(act)

                def take_transposed(step):
                    wait(act, t_pe, step)
                    act.activation(xT[:, :, :], ps[:, T0:T0 + 2, :], ACT.Copy).then_inc(t_act.sem, 1)
                    act.activation(xTh[:, :, :], ps[:, T0:T0 + 2, :], ACT.Copy).then_inc(t_act.sem, 1)

                def part(step, i, which):
                    dst, src = parts[i][step[1]], (rr, r1)[which][i]
                    if which == 0:
                        wait(act, qk_st, earlier(step, 2))
                        wait(act, rot_add, step, i + 1)
                    else:
                        wait(act, rest1, step, i + 1)
                    act.activation(dst[:, which], src[:, :, :], ACT.Copy).then_inc((part1, part2)[which].sem, 1)

                def values(step):
                    wait(act, v_st, earlier(step, 1))
                    wait(act, v_pe, step)
                    act.activation(vs[:, :, :, 0:DK].rearrange("p a h v -> p (a h) v"),
                                   ps[:, V0:V0 + 2, :].rearrange("p c (h v) -> p (c h) v", v=DK),
                                   ACT.Copy).then_inc(v_act.sem, 1)

                def gate(step, m):
                    wait(act, hid, *back2(step, m))
                    wait(act, gu_pe, step, m + 1)
                    act.activation(sg[:, m % 2], ps[:, (Q0, K0)[m % 2], :], ACT.Silu, scale=QSCALE).then_inc(silu.sem, 1)

                def high(step, m):
                    if m == 0:
                        wait(act, down_pe, earlier(step, 1))
                    wait(act, hid, step, m + 1)
                    act.activation(hh[:, m], h32[:, m % 2], ACT.Copy).then_inc(hid_hi.sem, 1)

                take_transposed((0, 0))

                def chunk(step, more):
                    part(step, 0, 0)
                    values(step)
                    part(step, 1, 0)
                    gate(step, 0)
                    gate(step, 1)
                    high(step, 0)
                    part(step, 0, 1)
                    gate(step, 2)
                    high(step, 1)
                    part(step, 1, 1)
                    for m in range(3, MH):
                        gate(step, m)
                        high(step, m - 1)
                    high(step, MH - 1)
                    if more:
                        take_transposed(nxt(step))
                    wait(act, g_st, earlier(step, 2))
                    for j in range(2):
                        wait(act, down_pe, step, j + 1)
                        act.activation(gs[:, step[1], 2 * j:2 * j + 2].rearrange("p a d -> p (a d)"), ps[:, V0 + j, :],
                                       ACT.Silu, scale=QSCALE / HSCALE).then_inc(gate_act.sem, 1)

                over_batches(act, chunk)

            @block.tensor
            def _(pe):
                for s in (t_pe, q_pe, k_pe, v_pe, gu_pe, down_pe):
                    s.start(pe)

                def transposes(step):
                    wait(pe, t_lo, earlier(step, 1))
                    wait(pe, ln_xn, step)
                    for kd in range(KD):
                        for a in range(CT):
                            ins = pe.transpose(ps[:, T0 + kd, a * P:(a + 1) * P], xn[:, a, kd * P:(kd + 1) * P], ident[:, :])
                    ins.then_inc(t_pe.sem, 1)

                transposes((0, 0))

                def chunk(step, more):
                    wait(pe, t_act, step)
                    for i, done in enumerate((q_pe, k_pe)):
                        wait(pe, hid, earlier(step, 1), MH - 1 + i)
                        for eo in range(2):
                            for kd in range(KD):
                                ins = pe.matmul(ps[:, (Q0, K0)[i] + eo, :], wqkT[:, kd, 2 * i + eo, :], xT[:, kd, :],
                                                start=kd == 0, stop=kd == KD - 1)
                        ins.then_inc(done.sem, 1)
                    wait(pe, gate_act, earlier(step, 1))
                    for a in range(CT):
                        for kd in range(KD):
                            ins = pe.matmul(ps[:, V0 + a // 2, (a % 2) * D:(a % 2 + 1) * D], xT[:, kd, a * P:(a + 1) * P],
                                            wvT[:, kd, :], start=kd == 0, stop=kd == KD - 1)
                    ins.then_inc(v_pe.sem, 1)
                    wait(pe, t_lo, step)
                    for m in range(MH):
                        if m < 2:
                            wait(pe, rot_mul, step, m + 1)
                        else:
                            wait(pe, hid, step, m - 1)
                        for gu in range(2):
                            n = 0
                            for kd in range(KD):
                                for xx in (xTh, xTl):
                                    ins = pe.matmul(ps[:, (Q0, K0)[m % 2] + gu, :], wguT[:, gu, kd, m * P:(m + 1) * P],
                                                    xx[:, kd, :], start=n == 0, stop=n == 2 * KD - 1)
                                    n += 1
                        ins.then_inc(gu_pe.sem, 1)
                    if more:
                        transposes(nxt(step))
                    wait(pe, v_act, step)
                    for a in range(CT):
                        for m in range(MH):
                            if a == 0:
                                wait(pe, hid_lo, step, m + 1)
                            for n, hx in enumerate((hh, hl)):
                                ins = pe.matmul(ps[:, V0 + a // 2, (a % 2) * D:(a % 2 + 1) * D], hx[:, m, a * P:(a + 1) * P],
                                                wdT[:, m, :], start=m == 0 and n == 0, stop=m == MH - 1 and n == 1)
                        if a % 2:
                            ins.then_inc(down_pe.sem, 1)

                over_batches(pe, chunk)



def score_units(by_key):
    units = []
    if by_key:
        for c in range(S // CH):
            for kb in range((c + 1) * CT):
                lo = max(kb * P, c * CH)
                w = (c + 1) * CH - lo
                n = min(GH, CH // w)
                units += [(kb, lo, w, tuple(range(h, h + n))) for h in range(0, GH, n)]
    else:
        for qb in range(QB):
            for lo in range(0, (qb + 1) * P, CH):
                w = min(CH, (qb + 1) * P - lo)
                n = 1 << ((CH // w).bit_length() - 1)
                n = min(GH, n)
                units += [(qb, lo, w, tuple(range(h, h + n))) for h in range(0, GH, n)]
    return units


def attention_phase(nc, ps, keep, scratch, attn_d):
    q_parts_d, k_parts_d, v_d = scratch
    ident = keep["ident"]
    MAXU, EXPU = score_units(False), score_units(True)
    NU = len(MAXU)
    assert NU == len(EXPU)
    SHIFT = 10
    NSTEP = sum((c + 1) * CT for c in range(S // CH))
    diag_units = [u for u, (kb, lo, w, hs) in enumerate(EXPU) if lo == kb * P]
    ND = len(diag_units)
    ctx = ExitStack()
    with ctx:
        sb = lambda n, s, d: ctx.enter_context(nc.sbuf_tensor(n, s, d))
        sem = lambda n: ctx.enter_context(nc.semaphore(n))
        stage = lambda n, k: Stage(ctx, nc, n, k, NG)

        ROWS = STACK + PARTS
        qs = [sb(f"qs{g}", [P, GH, S], BF16) for g in range(NG)]
        ks = [sb(f"ks{g}", [P, GH, S], BF16) for g in range(NG)]
        vt = [sb(f"vt{i}", [P, QB, GH, VW], F32) for i in range(2)]
        pr = [sb(f"pr{i}", [P, GH, CH], F32) for i in range(3)]
        mxa = [sb(f"mxa{i}", [P, GH, QB], F32) for i in range(2)]
        mxb = [sb(f"mxb{i}", [P, GH, QB // 2], F32) for i in range(2)]
        mneg = sb("mneg", [GH * QB, P], F32)
        mp = sb("mp", [GH * QB, PARTS, P], BF16)
        mr = sb("mr", [GH * QB, P], F32)
        ot = sb("ot", [P, 2, CH], F32)
        rec = sb("rec", [P, 2, CT * GH], F32)
        an = sb("an", [P, QB, GH, DK], F32)
        identb = sb("identb", [P, P], BF16)
        future = sb("future", [P, P], BF16)

        s_c = sem("s_c")
        s_held = sem("s_held2")
        s_cl = sem("s_cl")
        qk_ld = [sem(f"qk_ld{g}") for g in range(NG)]
        v_ld = [sem(f"v_ld{g}") for g in range(2)]
        max_pe, max_dve = stage("max_pe", NU), stage("max_dve", NU)
        mx_join, mx_t, mx_neg, mx_parts = stage("mx_join", 1), stage("mx_t", 1), stage("mx_neg", 1), stage("mx_parts", 4)
        mx_ld = stage("mx_ld", 16 * PARTS)
        st_pe, expo, causal = stage("st_pe", NU), stage("expo", NU), stage("causal", ND)
        pv_pe, o_act, o_pe = stage("pv_pe", NSTEP), stage("o_act", 2), stage("o_pe", 2)
        o_rec, o_norm, a_st = stage("o_rec", 2), stage("o_norm", 2), stage("a_st", 16)

        ST0, MX0, O0, M0 = 0, 3, 5, 7
        LOADS = 16 * 9

        q_v = q_parts_d.rearrange("b (r h) s -> b r h s", h=H)
        k_v = k_parts_d.rearrange("b (r h) s -> b r h s", h=H)
        a_v = attn_d.rearrange("b (q p) e -> b p q e", p=P)

        def nth(step, n):
            b, g = step
            return b + (g + n) // NG, (g + n) % NG

        def before_bank(units_k, step, u, nb):
            lst = [v for v in range(u) if v % nb == u % nb]
            if lst:
                return step, lst[-1] + 1
            lst = [v for v in range(units_k) if v % nb == u % nb]
            return earlier(step, 1), lst[-1] + 1

        with nc.Block() as block:

            def over_groups(eng, group):
                with eng.Fori(0, B - 1) as b:
                    for g in range(NG):
                        group((b, g), True)
                for g in range(NG):
                    group((B - 1, g), False)

            def maxima_of(step, more):
                b, g = step
                out = []
                if more or g + 1 < NG:
                    out += [(nth(step, 1), u) for u in range(SHIFT, NU)]
                if more or g + 2 < NG:
                    out += [(nth(step, 2), u) for u in range(SHIFT)]
                return out

            first_maxima = [((0, 0), u) for u in range(NU)] + [((0, 1), u) for u in range(SHIFT)]

            def key_step(u):
                kb, lo, w, hs = EXPU[u]
                c = lo // CH
                return (CT if c else 0) + kb if c else kb

            LAG = 5
            last_of = {}
            for u in range(NU):
                last_of[key_step(u)] = u
            O0_AT = last_of[CT - 1] + LAG + 3
            NORM0 = O0_AT + 3
            MAXT = NU - SHIFT + 2
            NEG = MAXT + 1

            def step_before(step, s, n):
                return (step, s - n + 1) if s >= n else (earlier(step, 1), NSTEP + s - n + 1)

            @block.sync
            def _(sp):
                mx_ld.start(sp)
                a_st.start(sp)
                sp.wait_ge(s_cl, 3)

                def load_stacks(step):
                    b, g = step
                    h = slice(g * GH, (g + 1) * GH)
                    sp.dma_start(qs[g][0:3 * DK], q_v[b, 0:3 * DK, h]).then_inc(qk_ld[g], 16)
                    sp.dma_start(qs[g][3 * DK:5 * DK], q_v[b, 0:2 * DK, h]).then_inc(qk_ld[g], 16)
                    sp.dma_start(qs[g][5 * DK:6 * DK], q_v[b, 0:DK, h]).then_inc(qk_ld[g], 16)
                    for n, part in enumerate(K_BANDS):
                        sp.dma_start(ks[g][n * DK:(n + 1) * DK], k_v[b, part * DK:(part + 1) * DK, h]).then_inc(qk_ld[g], 16)

                def load_v(step):
                    b, g = step
                    sp.dma_start(vt[g % 2].rearrange("p k h v -> p k (h v)")[:, :, :],
                                 v_d.rearrange("b k p e -> b p k e")[b, :, :, g * GH * VW:(g + 1) * GH * VW]).then_inc(v_ld[g % 2], 16)

                def load_max(step):
                    g = step[1]
                    wait(sp, st_pe, earlier(step, NG))
                    for part in range(PARTS):
                        wait(sp, mx_parts, step, (1, 3, 4)[part])
                        sp.dma_start(qs[g][STACK + part:STACK + part + 1].rearrange("p h (q s) -> p (h q) s", q=QB),
                                     mp[:, part, :]).then_inc(mx_ld.sem, 16)

                for g in range(NG - 1):
                    load_stacks((0, g))
                for g in range(2):
                    load_v((0, g))
                load_max((0, 0))

                def group(step, more):
                    b, g = step
                    nb, ng = nth(step, 3)
                    if more or ng > g:
                        wait(sp, st_pe, earlier((nb, ng), NG))
                        load_stacks((nb, ng))
                    if more or g < NG - 1:
                        load_max(nth(step, 1))
                    wait(sp, o_norm, step)
                    sp.dma_start(a_v[b, :, :, g * GH * DK:(g + 1) * GH * DK],
                                 an.rearrange("p q h e -> p q (h e)")[:, :, :]).then_inc(a_st.sem, 16)
                    if more or g < NG - 2:
                        wait(sp, pv_pe, step)
                        load_v(nth(step, 2))

                over_groups(sp, group)
                wait(sp, a_st, (B - 1, NG - 1))

            @block.gpsimd
            def _(pool):
                for s in (mx_parts, causal):
                    s.start(pool)
                ch = Chain(pool, s_c)
                ch(pool.memset(identb[:, :], 0.0))
                ch(pool.memset(future[:, :], 0.0))
                ch(pool.affine_select(out=identb[:, :], in_=identb[:, :], compare_op=ALU.not_equal, fill=1.0,
                                      base=0, pattern=[[-1, P]], channel_multiplier=1))
                ch(pool.affine_select(out=future[:, :], in_=future[:, :], compare_op=ALU.is_ge, fill=MASKED,
                                      base=0, pattern=[[-1, P]], channel_multiplier=1))

                def split_max(step):
                    wait(pool, mx_ld, earlier(step, 1))
                    wait(pool, mx_neg, step)
                    hold(pool, s_held)
                    pool.tensor_scalar(mp[:, 0], mneg[:, :], 1.0, 0.0, ALU.mult, ALU.add).then_inc(mx_parts.sem, 1)
                    wait(pool, mx_parts, step, 1)
                    pool.tensor_tensor(mr[:, :], mneg[:, :], mp[:, 0], ALU.subtract).then_inc(mx_parts.sem, 1)
                    wait(pool, mx_parts, step, 2)
                    hold(pool, s_held)
                    pool.tensor_scalar(mp[:, 1], mr[:, :], 1.0, 0.0, ALU.mult, ALU.add).then_inc(mx_parts.sem, 1)
                    wait(pool, mx_parts, step, 3)
                    pool.tensor_tensor(mp[:, 2], mr[:, :], mp[:, 1], ALU.subtract).then_inc(mx_parts.sem, 1)

                def mask(step, n):
                    kb, lo, w, hs = EXPU[diag_units[n]]
                    s = key_step(diag_units[n])
                    blk = pr[s % 3][:, hs[0]:hs[-1] + 1, 0:P]
                    wait(pool, expo, step, diag_units[n] + 1)
                    hold(pool, s_held)
                    pool.affine_select(out=blk, in_=blk, compare_op=ALU.is_ge, fill=0.0, base=0,
                                       pattern=[[0, len(hs)], [1, P]], channel_multiplier=-1).then_inc(causal.sem, 1)

                split_max((0, 0))

                def group(step, more):
                    where = NU - 4
                    done = False
                    for n in range(ND):
                        if not done and diag_units[n] > where:
                            done = True
                            if more or step[1] + 1 < NG:
                                split_max(nth(step, 1))
                        mask(step, n)
                    if not done and (more or step[1] + 1 < NG):
                        split_max(nth(step, 1))

                over_groups(pool, group)

            def maximum(dve, step, u):
                qb, lo, w, hs = MAXU[u]
                par = step[1] % 2
                dst = mxa[par][:, hs[0]:hs[-1] + 1, qb] if lo == 0 else mxb[par][:, hs[0]:hs[-1] + 1, qb - QB // 2]
                if u == 0:
                    wait(dve, mx_t, earlier(step, 2))
                    wait(dve, mx_join, earlier(step, 2))
                wait(dve, max_pe, step, u + 1)
                dve.tensor_reduce(dst, ps[:, MX0 + u % 2, 0:w * len(hs)].rearrange("p (h s) -> p h s", s=w),
                                  axis=AX.X, op=ALU.max).then_inc(max_dve.sem, 1)

            def join_max(dve, step):
                par = step[1] % 2
                wait(dve, max_dve, step)
                dve.tensor_tensor(mxa[par][:, :, QB // 2:], mxa[par][:, :, QB // 2:], mxb[par][:, :, :],
                                  ALU.max).then_inc(mx_join.sem, 1)

            def negate_max(dve, step):
                wait(dve, mx_parts, earlier(step, 1))
                wait(dve, mx_t, step)
                dve.tensor_scalar(mneg[:, :], ps[0:GH * QB, M0, 0:P], -1.0, None, ALU.mult).then_inc(mx_neg.sem, 1)

            @block.vector
            def _(dve):
                for s in (max_dve, mx_join, mx_neg, o_rec, o_norm):
                    s.start(dve)
                for g in range(NG):
                    dve.memset(ks[g][STACK:ROWS], 1.0)
                    dve.memset(qs[g][STACK:ROWS], 0.0)
                dve.memset(mxb[0][:, :, :], 0.0).then_inc(s_cl, 3)

                def normalise(step, c):
                    o = ps[:, M0, :].rearrange("p (r v) -> p r v", v=VW)
                    if c == 0:
                        wait(dve, a_st, earlier(step, 1))
                    wait(dve, o_norm, earlier(step, 1), c + 1)
                    wait(dve, o_pe, step, c + 1)
                    dve.reciprocal(rec[:, c], o[:, :, DK]).then_inc(o_rec.sem, 1)
                    wait(dve, o_rec, step, c + 1)
                    dve.tensor_tensor(an[:, c * CT:(c + 1) * CT].rearrange("p q h e -> p (q h) e"), o[:, :, 0:DK],
                                      rec[:, c].unsqueeze(2).to_broadcast([P, CT * GH, DK]), ALU.mult).then_inc(o_norm.sem, 1)

                for ms, u in first_maxima:
                    maximum(dve, ms, u)
                    if u == NU - 1:
                        join_max(dve, ms)
                negate_max(dve, (0, 0))

                def group(step, more):
                    todo = maxima_of(step, more)
                    for n in range(NU):
                        if n < len(todo):
                            ms, u = todo[n]
                            maximum(dve, ms, u)
                            if u == NU - 1:
                                join_max(dve, ms)
                        if n == NORM0:
                            normalise(step, 0)
                        if n == NEG and (more or step[1] + 1 < NG):
                            negate_max(dve, nth(step, 1))
                    normalise(step, 1)

                over_groups(dve, group)

            @block.scalar
            def _(act):
                for s in (expo, o_act):
                    s.start(act)

                def exponentials(step, u):
                    kb, lo, w, hs = EXPU[u]
                    s = key_step(u)
                    prev = step_before(step, s, 3)
                    wait(act, pv_pe, *prev)
                    wait(act, st_pe, step, u + 1)
                    act.activation(pr[s % 3][:, hs[0]:hs[-1] + 1, 0:w],
                                   ps[:, ST0 + u % 3, 0:w * len(hs)].rearrange("p (h s) -> p h s", s=w),
                                   ACT.Exp, scale=1.0 / DK ** 0.5).then_inc(expo.sem, 1)

                def take_output(step, c):
                    wait(act, o_pe, earlier(step, 1), c + 1)
                    wait(act, pv_pe, step, CT if c == 0 else NSTEP)
                    act.activation(ot[:, c], ps[:, O0 + c, :], ACT.Copy).then_inc(o_act.sem, 1)

                def group(step, more):
                    for u in range(NU):
                        exponentials(step, u)
                        if u == O0_AT - 2:
                            take_output(step, 0)
                    take_output(step, 1)

                over_groups(act, group)

            @block.tensor
            def _(pe):
                for s in (max_pe, mx_t, st_pe, pv_pe, o_pe):
                    s.start(pe)
                pe.wait_ge(s_c, 4)
                pe.wait_ge(s_cl, 3)

                def queries_by_keys(step, u):
                    qb, lo, w, hs = MAXU[u]
                    b, g = step
                    if u == 0:
                        pe.wait_ge(qk_ld[g], b * LOADS + LOADS)
                    wait(pe, max_dve, *before_bank(NU, step, u, 2))
                    diag = lo + w > qb * P
                    for n, h in enumerate(hs):
                        o = ps[:, MX0 + u % 2, n * w:(n + 1) * w]
                        ins = pe.matmul(o, qs[g][0:STACK, h, qb * P:(qb + 1) * P], ks[g][0:STACK, h, lo:lo + w],
                                        start=n == 0, stop=not diag, skip_group_check=True)
                        if diag:
                            ins = pe.matmul(o[:, w - P:w], identb[:, :], future[:, :], start=False, stop=True,
                                            skip_group_check=True)
                    ins.then_inc(max_pe.sem, 1)

                def keys_by_queries(step, u):
                    kb, lo, w, hs = EXPU[u]
                    g = step[1]
                    if u == 0:
                        wait(pe, mx_ld, step)
                    wait(pe, expo, *before_bank(NU, step, u, 3))
                    for n, h in enumerate(hs):
                        ins = pe.matmul(ps[:, ST0 + u % 3, n * w:(n + 1) * w], ks[g][0:ROWS, h, kb * P:(kb + 1) * P],
                                        qs[g][0:ROWS, h, lo:lo + w], start=True, stop=True)
                    ins.then_inc(st_pe.sem, 1)

                def times_v(step, s):
                    b, g = step
                    c = 0 if s < CT else 1
                    kb = s if s < CT else s - CT
                    lo = max(kb * P - c * CH, 0)
                    if s == 0:
                        pe.wait_ge(v_ld[g % 2], b * 32 + 16 * (g // 2) + 16)
                    if kb == 0:
                        wait(pe, o_act, earlier(step, 1), c + 1)
                    nd = [n for n, u in enumerate(diag_units) if key_step(u) == s]
                    if nd:
                        wait(pe, causal, step, nd[-1] + 1)
                    wait(pe, expo, step, last_of[s] + 1)
                    for j in range(GH):
                        ins = pe.matmul(ps[VW * j:VW * (j + 1), O0 + c, lo:CH], vt[g % 2][:, kb, j, :],
                                        pr[s % 3][:, j, 0:CH - lo], start=kb == 0, stop=kb == (c + 1) * CT - 1)
                    ins.then_inc(pv_pe.sem, 1)

                def transpose_max(step):
                    wait(pe, o_norm, earlier(step, 1), 1)
                    wait(pe, mx_join, step)
                    pe.matmul(ps[0:GH * QB, M0, 0:P], mxa[step[1] % 2].rearrange("p h q -> p (h q)")[:, :], ident[:, :],
                              start=True, stop=True).then_inc(mx_t.sem, 1)

                def transpose_output(step, c, more):
                    if c == 0:
                        wait(pe, mx_neg, step)
                        wait(pe, o_norm, earlier(step, 1))
                    elif more or step[1] + 1 < NG:
                        wait(pe, mx_neg, nth(step, 1))
                    else:
                        wait(pe, o_norm, step, 1)
                    wait(pe, o_act, step, c + 1)
                    for a in range(CT):
                        ins = pe.transpose(ps[:, M0, a * P:(a + 1) * P], ot[:, c, a * P:(a + 1) * P], ident[:, :])
                    ins.then_inc(o_pe.sem, 1)

                for ms, u in first_maxima:
                    queries_by_keys(ms, u)
                transpose_max((0, 0))

                def group(step, more):
                    todo = maxima_of(step, more)
                    pending = list(range(NSTEP))
                    for n in range(NU):
                        keys_by_queries(step, n)
                        if n < len(todo):
                            queries_by_keys(*todo[n])
                        while pending and last_of[pending[0]] + LAG <= n:
                            times_v(step, pending.pop(0))
                        if n == O0_AT:
                            transpose_output(step, 0, more)
                        if n == MAXT and (more or step[1] + 1 < NG):
                            transpose_max(nth(step, 1))
                    for s in pending:
                        times_v(step, s)
                    transpose_output(step, 1, more)

                over_groups(pe, group)


def output_phase(nc, ps, keep, x, gate_d, attn_d, out):
    ident, woT = keep["ident"], keep["woT"]
    ctx = ExitStack()
    with ctx:
        sb = lambda n, s, d: ctx.enter_context(nc.sbuf_tensor(n, s, d))
        stage = lambda n, k: Stage(ctx, nc, n, k, HALVES)
        at = sb("at", [P, 2, CT, D], F32)
        gt = sb("gt", [P, 2, CT, D], F32)
        xt = sb("xt", [P, 2, CT, D], F32)
        aT = sb("aT", [P, 2, KD, CH], F32)
        yt = sb("yt", [P, 2, CT, D], F32)
        zt = sb("zt", [P, 2, CT, D], F32)
        ld = [ctx.enter_context(nc.semaphore(f"o_ld{i}")) for i in range(2)]
        tr, ev, wo_pe, mul, add = (stage(n, 1) for n in ("o_tr", "o_ev", "o_wo", "o_mul", "o_add"))
        st = [Stage(ctx, nc, f"o_st{i}", 16, 1) for i in range(2)]
        view = lambda d: d.rearrange("b (c a p) d -> b c p a d", c=HALVES, p=P)
        sources = ((view(attn_d), at), (view(gate_d), gt), (view(x), xt))

        with nc.Block() as block:

            def over(eng, chunk):
                with eng.Fori(0, B) as b:
                    for c in range(HALVES):
                        chunk((b, c))

            @block.sync
            def _(sp):
                def chunk(step):
                    b, c = step
                    wait(sp, add, earlier(step, 2))
                    for src, dst in sources:
                        sp.dma_start(dst[:, c], src[b, c]).then_inc(ld[c], 16)
                over(sp, chunk)

            @block.gpsimd
            def _(pool):
                add.start(pool)

                def chunk(step):
                    b, c = step
                    wait(pool, st[c], (b, -1))
                    wait(pool, mul, step)
                    pool.tensor_tensor(zt[:, c], yt[:, c], xt[:, c], ALU.add).then_inc(add.sem, 1)
                over(pool, chunk)

            @block.scalar
            def _(act):
                ev.start(act)
                for s in st:
                    s.start(act)

                def chunk(step):
                    b, c = step
                    wait(act, wo_pe, earlier(step, 2))
                    wait(act, tr, step)
                    act.activation(aT[:, c], ps[:, 2 * c:2 * c + 2, :], ACT.Copy).then_inc(ev.sem, 1)
                    wait(act, add, step)
                    act.dma_start(view(out)[b, c], zt[:, c]).then_inc(st[c].sem, 16)
                over(act, chunk)
                for s in st:
                    wait(act, s, (B - 1, 0))

            @block.vector
            def _(dve):
                mul.start(dve)

                def chunk(step):
                    c = step[1]
                    wait(dve, add, earlier(step, 2))
                    wait(dve, wo_pe, step)
                    dve.tensor_tensor(yt[:, c].rearrange("p (t a) d -> p t (a d)", t=2), ps[:, 4 + 2 * c:6 + 2 * c, :],
                                      gt[:, c].rearrange("p (t a) d -> p t (a d)", t=2), ALU.mult).then_inc(mul.sem, 1)
                over(dve, chunk)

            @block.tensor
            def _(pe):
                tr.start(pe)
                wo_pe.start(pe)

                def chunk(step):
                    b, c = step
                    pe.wait_ge(ld[c], b * 48 + 48)
                    wait(pe, ev, earlier(step, 2))
                    for kd in range(KD):
                        for a in range(CT):
                            ins = pe.transpose(ps[:, 2 * c + kd, a * P:(a + 1) * P], at[:, c, a, kd * P:(kd + 1) * P], ident[:, :])
                    ins.then_inc(tr.sem, 1)
                    wait(pe, mul, earlier(step, 2))
                    wait(pe, ev, step)
                    for a in range(CT):
                        for kd in range(KD):
                            ins = pe.matmul(ps[:, 4 + 2 * c + a // 2, (a % 2) * D:(a % 2 + 1) * D],
                                            aT[:, c, kd, a * P:(a + 1) * P], woT[:, kd, :], start=kd == 0, stop=kd == KD - 1)
                    ins.then_inc(wo_pe.sem, 1)
                over(pe, chunk)


def program(nc, x, wq, wk, wv, wo, w_gate, w_up, w_down, cs, out):
    nc.disable_value_cache = True
    q_parts_d = nc.dram_tensor("q_parts_d", [B, PARTS * 2 * P, S], BF16).ap()
    k_parts_d = nc.dram_tensor("k_parts_d", [B, PARTS * 2 * P, S], BF16).ap()
    v_d = nc.dram_tensor("v_d", [B, QB, P, H * VW], F32).ap()
    gate_d = nc.dram_tensor("gate_d", [B, S, D], F32).ap()
    attn_d = nc.dram_tensor("attn_d", [B, S, D], F32).ap()
    with ExitStack() as ctx:
        ps = ctx.enter_context(nc.psum_tensor("ps", [P, 8, 512], F32))
        keep = {"ident": ctx.enter_context(nc.sbuf_tensor("ident", [P, P], F32)),
                "woT": ctx.enter_context(nc.sbuf_tensor("woT", [P, KD, D], F32))}
        project_phase(nc, ps, keep, x, wq, wk, wv, wo, w_gate, w_up, w_down, cs, (q_parts_d, k_parts_d, v_d, gate_d))
        attention_phase(nc, ps, keep, (q_parts_d, k_parts_d, v_d), attn_d)
        output_phase(nc, ps, keep, x, gate_d, attn_d, out)


_INS = ["L0_attn_x", "L0_attn_wq", "L0_attn_wk", "L0_attn_wv", "L0_attn_wo", "L0_ffn_w_gate", "L0_ffn_w_up", "L0_ffn_w_down"]


def kernel(**inputs):
    import numpy as _np
    import concourse.bacc as _bacc
    from concourse import mybir as _mybir
    from concourse.bass_utils import run_bass_kernel_spmd as _run

    nc = _bacc.Bacc("TRN2", target_bir_lowering=False, num_devices=1)
    arrays, args = {}, []
    for name in _INS:
        a = _np.ascontiguousarray(inputs[name])
        arrays[f"in_{name}"] = a
        args.append(nc.dram_tensor(f"in_{name}", a.shape, _mybir.dt.from_np(a.dtype), kind="ExternalInput").ap())
    f = _np.float32
    angle = _np.arange(S, dtype=f)[:, None] / f(10000.0) ** (f(2.0) * _np.arange(PAIRS, dtype=f)[None, :] / f(DK))
    sin, cos = (_np.repeat(t(angle).T, H, axis=0) for t in (_np.sin, _np.cos))
    a = _np.ascontiguousarray(_np.stack([_np.stack([cos, -sin], 1), _np.stack([sin, cos], 1)], 1))
    arrays["in_trig"] = a
    args.append(nc.dram_tensor("in_trig", a.shape, F32, kind="ExternalInput").ap())
    args.append(nc.dram_tensor("out_dram", (B, S, D), F32, kind="ExternalOutput").ap())
    program(nc, *args)
    r = _run(nc, [arrays], core_ids=[0])
    return r.results[0]["out_dram"]
```

```python
import concourse.bass as bass
from concourse import mybir
from contextlib import ExitStack

F32 = mybir.dt.float32
F16 = mybir.dt.float16
BF16 = mybir.dt.bfloat16
I32 = mybir.dt.int32
ACT = mybir.ActivationFunctionType
ALU = mybir.AluOpType
AX = mybir.AxisListType

P = 128
B, S, D = 8, 1024, 256
H, DK = 16, 16
HID = 768
EPS = 1e-5
QSCALE = 1.0 / 127.0
HSCALE = 0.125
KD = D // P
MH = HID // P
CH = 512
CT = CH // P
HALVES = S // CH
PAIRS = DK // 2
GH = 4
NG = H // GH
QB = S // P
VW = 32
PARTS = 3
STACK = 6 * DK
MASKED = -3.0e38
ONES_TWICE = 1.0 + 0x3F80 * 2.0 ** -23
Q_BANDS = (0, 1, 2, 0, 1, 0)
K_BANDS = (0, 0, 0, 1, 1, 2)


class Stage:

    def __init__(self, ctx, nc, name, k, per):
        self.sem = ctx.enter_context(nc.semaphore(name))
        self.k, self.per = k, per
        self.lead = per + 2

    def start(self, eng):
        eng.sem_inc(self.sem, self.lead * self.k)

    def after(self, step, count=None):
        loop, off = step
        count = self.k if count is None else count
        return loop * (self.per * self.k) + ((off + self.lead) * self.k + count)


def wait(eng, stage, step, count=None):
    eng.wait_ge(stage.sem, stage.after(step, count))


def hold(eng, sem):
    eng.sem_inc(sem, 1)


def earlier(step, n):
    return step[0], step[1] - n


class Chain:

    def __init__(self, eng, sem):
        self.eng, self.sem, self.n = eng, sem, 0

    def __call__(self, instruction):
        instruction.then_inc(self.sem, 1)
        self.n += 1
        self.eng.wait_ge(self.sem, self.n)


def project_phase(nc, ps, keep, x, wq, wk, wv, wo, w_gate, w_up, w_down, cs, scratch):
    q_parts_d, k_parts_d, v_d, gate_d = scratch
    ident, woT = keep["ident"], keep["woT"]
    ctx = ExitStack()
    with ctx:
        sb = lambda n, s, d: ctx.enter_context(nc.sbuf_tensor(n, s, d))
        sem = lambda n: ctx.enter_context(nc.semaphore(n))
        stage = lambda n, k: Stage(ctx, nc, n, k, HALVES)

        wqkT = sb("wqkT", [P, KD, 4, P], F32)
        wvT = sb("wvT", [P, KD, D], F32)
        wguT = sb("wguT", [P, 2, KD, HID], F16)
        wdT = sb("wdT", [P, MH, D], F16)
        trig = sb("trig", [P, 2, 2, S], F32)
        negh = sb("negh", [P, CT], F32)

        xs = sb("xs", [P, 2, CT, D], F32)
        st = sb("st", [P, CT, 6], F32)
        mv = sb("mv", [P, CT, 2], F32)
        ve = sb("ve", [P, CT], F32)
        rstd = sb("rstd", [P, CT], F32)
        xn = sb("xn", [P, CT, D], F32)
        xT = sb("xT", [P, KD, CH], F32)
        xTh = sb("xTh", [P, KD, CH], F16)
        xTl = sb("xTl", [P, KD, CH], F16)
        gs = sb("gs", [P, 2, CT, D], F32)
        vs = sb("vs", [P, CT, H, VW], F32)

        s_const = sem("s_const")
        s_one = sem("s_one")
        s_held = sem("s_held")
        s_wload = sem("s_wload")
        s_iload = [sem(f"s_iload{i}") for i in range(3)]
        s_prep = sem("s_prep")
        s_wt = sem("s_wt")
        s_we = [sem(f"s_we{i}") for i in range(2)]
        x_ld = [stage(f"x_ld{i}", 0) for i in range(2)]
        ln_stat, ln_aggr = stage("ln_stat", 1), stage("ln_aggr", 1)
        ln_ve, ln_rs, ln_xn = stage("ln_ve", 1), stage("ln_rs", 1), stage("ln_xn", 1)
        t_pe, t_act, t_lo = stage("t_pe", 1), stage("t_act", 2), stage("t_lo", 1)
        q_pe, k_pe, v_pe = stage("q_pe", 1), stage("k_pe", 1), stage("v_pe", 1)
        rot_mul, rot_add = stage("rot_mul", 2), stage("rot_add", 2)
        part1, part2, part3 = stage("part1", 2), stage("part2", 2), stage("part3", 2)
        rest1 = stage("rest1q", 1), stage("rest1k", 1)
        v_act = stage("v_act", 1)
        gu_pe, silu, hid = stage("gu_pe", MH), stage("silu", MH), stage("hid", MH)
        LOW_POOL = 5
        hid_hi = stage("hid_hi", MH)
        lo_pool, lo_dve = stage("lo_pool", LOW_POOL), stage("lo_dve", MH - LOW_POOL)
        down_pe, gate_act = stage("down_pe", 2), stage("gate_act", 2)
        qk_st, v_st, g_st = stage("qk_st", 32), stage("v_st", 16), stage("g_st", 16)

        T0, Q0, K0, V0 = 0, 2, 4, 6
        FFN = (Q0, K0, V0, Q0, K0, Q0)

        x_v = x.rearrange("b (c a p) d -> b c p a d", c=HALVES, p=P)

        with ExitStack() as pre, nc.Block() as block:
            raw = pre.enter_context(nc.sbuf_tensor("raw", [P, 8, D], F32))
            rawi = pre.enter_context(nc.sbuf_tensor("rawi", [P, 18, D], I32))
            rawf = pre.enter_context(nc.sbuf_tensor("rawf", [P, 18, D], F32))

            @block.sync
            def _(sp):
                for i, w in enumerate((wq, wk, wv, wo)):
                    sp.dma_start(raw[:, 2 * i:2 * i + 2, :], w.rearrange("(m p) d -> p m d", p=P)).then_inc(s_wload, 16)
                sp.dma_start(xs[:, 0], x_v[0, 0]).then_inc(x_ld[0].sem, 16)
                for i, w in enumerate((w_gate, w_up)):
                    sp.dma_start(rawi[:, 6 * i:6 * i + 6, :], w.rearrange("(m p) d -> p m d", p=P)).then_inc(s_iload[i], 16)
                sp.dma_start(rawi[:, 12:18, :].rearrange("p (a m) e -> p a (m e)", a=2),
                             w_down.rearrange("(a p) e -> p a e", p=P)).then_inc(s_iload[2], 16)
                sp.dma_start(xs[:, 1], x_v[0, 1]).then_inc(x_ld[1].sem, 16)
                sp.dma_start(trig[:, :, :, :], cs[:, :, :, :]).then_inc(s_const, 16)

            @block.gpsimd
            def _(pool):
                ch = Chain(pool, s_prep)
                ch(pool.memset(ident[:, :], 0.0))
                ch(pool.affine_select(out=ident[:, :], in_=ident[:, :], compare_op=ALU.not_equal, fill=1.0,
                                      base=0, pattern=[[-1, P]], channel_multiplier=1))
                ch(pool.memset(negh[:, :], -0.5))
                ch(pool.memset(vs[:, :, :, :], 0.0))
                ch(pool.memset(vs[:, :, :, DK:DK + 1], 1.0))

            banks = []
            for i in range(2):
                banks.append(([raw[:, 2 * i + m, kd * P:(kd + 1) * P] for kd in range(KD) for m in range(2)],
                              [(wqkT[:, kd, 2 * i + eo, :].rearrange("p (i h) -> p i h", h=H), kd, eo)
                               for kd in range(KD) for eo in range(2)]))
            for i, dst in ((2, wvT), (3, woT)):
                banks.append(([raw[:, 2 * i + m, kd * P:(kd + 1) * P] for kd in range(KD) for m in range(2)],
                              [(dst[:, :, :].rearrange("p k e -> p (k e)"), None, None)]))
            n_float = len(banks)
            for gu in range(2):
                for kd in range(KD):
                    for m in range(0, MH, 2):
                        banks.append(([rawf[:, 6 * gu + mm, kd * P:(kd + 1) * P] for mm in (m, m + 1)],
                                      [(wguT[:, gu, kd, m * P:(m + 2) * P], None, None)]))
            down = rawf[:, 12:18, :].rearrange("p (a m) e -> p a (m e)", a=2)
            for m in range(0, MH, 2):
                banks.append(([down[:, a, mm * P:(mm + 1) * P] for mm in (m, m + 1) for a in range(2)],
                              [(wdT[:, m:m + 2, :].rearrange("p m d -> p (m d)"), None, None)]))

            def evacuate(eng, copy, n):
                srcs, dsts = banks[n]
                eng.wait_ge(s_wt, n + 1)
                for dst, kd, eo in dsts:
                    if kd is None:
                        src = ps[:, n % 8, 0:P * len(srcs)]
                    else:
                        src = ps[:, n % 8, kd * D:(kd + 1) * D].rearrange("p (h i two) -> p two i h", i=PAIRS, two=2)[:, eo]
                    ins = copy(dst, src)
                ins.then_inc(s_we[n % 2], 1)

            @block.vector
            def _(dve):
                for n in range(0, n_float, 2):
                    evacuate(dve, dve.tensor_copy, n)
                for i in range(3):
                    dve.wait_ge(s_iload[i], 16)
                    dve.tensor_copy(rawf[:, 6 * i:6 * i + 6], rawi[:, 6 * i:6 * i + 6]).then_inc(s_one, 1)
                for n in range(n_float, len(banks), 2):
                    evacuate(dve, dve.tensor_copy, n)

            @block.scalar
            def _(act):
                for n in range(1, len(banks), 2):
                    evacuate(act, lambda dst, src: act.activation(dst, src, ACT.Copy), n)

            @block.tensor
            def _(pe):
                pe.wait_ge(s_prep, 2)
                pe.wait_ge(s_wload, 16 * 4)
                for n, (srcs, _) in enumerate(banks):
                    if n >= n_float:
                        pe.wait_ge(s_one, 1 + (n - n_float) // MH)
                    if n >= 8:
                        pe.wait_ge(s_we[n % 2], n // 2 - 3)
                    for j, src in enumerate(srcs):
                        ins = pe.transpose(ps[:, n % 8, j * P:(j + 1) * P], src, ident[:, :])
                    ins.then_inc(s_wt, 1)

        tq = [sb(f"rot{i}", [P, 2, 2, CH], F32) for i in range(2)]
        rr = [sb(f"rr{i}", [P, 2, CH], F32) for i in range(2)]
        r1 = [sb(f"r1{i}", [P, 2, CH], F32) for i in range(2)]
        parts = [[sb(f"parts{i}{j}", [P, PARTS, 2, CH], BF16) for j in range(2)] for i in range(2)]
        NH = 4
        sg = sb("sg", [P, NH, CH], F32)
        h32 = sb("h32", [P, NH, CH], F32)
        hh = sb("hh", [P, MH, CH], F16)
        hl = sb("hl", [P, MH, CH], F16)

        qk_dst = [d.rearrange("b (r p) s -> b p r s", p=P) for d in (q_parts_d, k_parts_d)]
        gate_v = gate_d.rearrange("b (c a p) d -> b c p a d", c=HALVES, p=P)
        v_v = v_d.rearrange("b (c a) p e -> b c p a e", c=HALVES)

        with nc.Block() as block:

            def over_batches(eng, chunk):
                with eng.Fori(0, B - 1) as b:
                    for c in range(HALVES):
                        chunk((b, c), True)
                for c in range(HALVES):
                    chunk((B - 1, c), c + 1 < HALVES)

            @block.sync
            def _(sp):
                for s in (qk_st, v_st, g_st):
                    s.start(sp)
                def chunk(step, more):
                    b, c = step
                    if isinstance(b, int):
                        ahead = False
                    else:
                        ahead = True
                    if ahead:
                        wait(sp, ln_xn, step)
                        sp.dma_start(xs[:, c], x_v[b + 1, c]).then_inc(x_ld[c].sem, 16)
                    for i in range(2):
                        wait(sp, part3, step, i + 1)
                        sp.dma_start(qk_dst[i][b, :, :, c * CH:(c + 1) * CH],
                                     parts[i][c].rearrange("p a e s -> p (a e) s")[:, :, :]).then_inc(qk_st.sem, 16)
                    wait(sp, v_act, step)
                    sp.dma_start(v_v[b, c], vs.rearrange("p a h v -> p a (h v)")[:, :, :]).then_inc(v_st.sem, 16)
                    wait(sp, gate_act, step)
                    sp.dma_start(gate_v[b, c], gs[:, c]).then_inc(g_st.sem, 16)

                over_batches(sp, chunk)
                last = (B - 1, HALVES - 1)
                for s in (qk_st, v_st, g_st):
                    wait(sp, s, last)

            def slot_user(step, m):
                return (step, m - NH) if m >= NH else (earlier(step, 1), MH + m - NH)

            def wait_low(eng, step, m):
                if m < LOW_POOL:
                    wait(eng, lo_pool, step, m + 1)
                else:
                    wait(eng, lo_dve, step, m - LOW_POOL + 1)

            def rest(eng, step, i):
                wait(eng, part2, earlier(step, 1), i + 1)
                wait(eng, part3, earlier(step, 1), i + 1)
                wait(eng, rot_add, step, i + 1)
                wait(eng, part1, step, i + 1)
                eng.tensor_tensor(r1[i][:, :, :], rr[i][:, :, :], parts[i][step[1]][:, 0], ALU.subtract).then_inc(rest1[i].sem, 1)

            def low(eng, step, m):
                if m in (0, LOW_POOL):
                    wait(eng, down_pe, earlier(step, 1))
                wait(eng, hid_hi, step, m + 1)
                eng.tensor_tensor(hl[:, m], h32[:, m % NH], hh[:, m], ALU.subtract).then_inc((lo_pool if m < LOW_POOL else lo_dve).sem, 1)

            def x_arrived(eng, step):
                b, c = step
                if c >= HALVES:
                    b, c = b + 1, c - HALVES
                eng.wait_ge(x_ld[c].sem, b * 16 + 16)
                return c

            def nxt(step):
                return step[0], step[1] + 1

            @block.vector
            def _(dve):
                for s in (ln_stat, ln_aggr, ln_xn, t_lo, rot_mul, part3, hid, rest1[0], lo_dve):
                    s.start(dve)

                def stats(step):
                    c = x_arrived(dve, step)
                    wait(dve, ln_aggr, earlier(step, 1))
                    for a in range(CT):
                        ins = dve.bn_stats(st[:, a], xs[:, c, a])
                    ins.then_inc(ln_stat.sem, 1)
                    wait(dve, ln_rs, earlier(step, 1))
                    wait(dve, ln_xn, earlier(step, 1))
                    wait(dve, ln_stat, step)
                    hold(dve, s_held)
                    for a in range(CT):
                        ins = dve.bn_aggr(mv[:, a], st[:, a])
                    ins.then_inc(ln_aggr.sem, 1)

                def normalise(step):
                    c = step[1] % HALVES
                    wait(dve, t_pe, earlier(step, 1))
                    wait(dve, ln_rs, step)
                    for a in range(CT):
                        ins = dve.tensor_scalar(xn[:, a], xs[:, c, a], mv[:, a, 0:1], rstd[:, a:a + 1],
                                                ALU.subtract, ALU.mult)
                    ins.then_inc(ln_xn.sem, 1)

                def low_part(step):
                    wait(dve, t_act, step)
                    dve.tensor_tensor(xTl[:, :, :], ps[:, T0:T0 + 2, :], xTh[:, :, :], ALU.subtract).then_inc(t_lo.sem, 1)

                dve.wait_ge(s_const, 16)

                def rotate(step, i, pe_stage):
                    c = step[1]
                    wait(dve, rot_add, earlier(step, 1), i + 1)
                    wait(dve, pe_stage, step)
                    for t in range(2):
                        ins = dve.tensor_tensor(tq[i][:, t], ps[:, (Q0, K0)[i]:(Q0, K0)[i] + 2, :],
                                                trig[:, t, :, c * CH:(c + 1) * CH], ALU.mult)
                    ins.then_inc(rot_mul.sem, 1)

                def third_part(step, i):
                    wait(dve, part2, step, i + 1)
                    dve.tensor_tensor(parts[i][step[1]][:, 2], r1[i][:, :, :], parts[i][step[1]][:, 1],
                                      ALU.subtract).then_inc(part3.sem, 1)

                def hidden(step, m):
                    before, mb = slot_user(step, m)
                    wait(dve, hid_hi, before, mb + 1)
                    wait_low(dve, before, mb)
                    wait(dve, silu, step, m + 1)
                    dve.scalar_tensor_tensor(out=h32[:, m % NH], in0=ps[:, FFN[m] + 1, :], scalar=QSCALE * HSCALE,
                                             in1=sg[:, m % NH], op0=ALU.mult, op1=ALU.mult).then_inc(hid.sem, 1)

                stats((0, 0))
                normalise((0, 0))
                low_part((0, 0))

                def chunk(step, more):
                    rotate(step, 0, q_pe)
                    rotate(step, 1, k_pe)
                    rest(dve, step, 0)
                    if more:
                        stats(nxt(step))
                    hidden(step, 0)
                    hidden(step, 1)
                    if more:
                        normalise(nxt(step))
                    hidden(step, 2)
                    third_part(step, 0)
                    hidden(step, 3)
                    hidden(step, 4)
                    third_part(step, 1)
                    hidden(step, 5)
                    for m in range(LOW_POOL, MH):
                        low(dve, step, m)
                    if more:
                        low_part(nxt(step))

                over_batches(dve, chunk)

            @block.gpsimd
            def _(pool):
                for s in (ln_ve, ln_rs, rot_add, rest1[1], lo_pool):
                    s.start(pool)

                def inverse_root(step):
                    wait(pool, ln_xn, earlier(step, 1))
                    wait(pool, ln_aggr, step)
                    hold(pool, s_held)
                    pool.tensor_scalar(ve[:, :], mv[:, :, 1], EPS, 1.0, ALU.add, ALU.mult).then_inc(ln_ve.sem, 1)
                    wait(pool, ln_ve, step)
                    pool.tensor_tensor(rstd[:, :], ve[:, :], negh[:, :], ALU.pow).then_inc(ln_rs.sem, 1)

                def rotated(step, i):
                    wait(pool, part1, earlier(step, 1), i + 1)
                    wait(pool, rest1[i], earlier(step, 1))
                    wait(pool, rot_mul, step, i + 1)
                    pool.tensor_tensor(rr[i][:, :, :], tq[i][:, :, 0, :], tq[i][:, :, 1, :], ALU.add).then_inc(rot_add.sem, 1)

                inverse_root((0, 0))

                def chunk(step, more):
                    rotated(step, 0)
                    rotated(step, 1)
                    if more:
                        inverse_root(nxt(step))
                    rest(pool, step, 1)
                    for m in range(LOW_POOL):
                        low(pool, step, m)

                over_batches(pool, chunk)

            @block.scalar
            def _(act):
                for s in (t_act, part1, part2, v_act, silu, hid_hi, gate_act):
                    s.start(act)

                def take_transposed(step):
                    wait(act, t_pe, step)
                    act.activation(xT[:, :, :], ps[:, T0:T0 + 2, :], ACT.Copy).then_inc(t_act.sem, 1)
                    act.activation(xTh[:, :, :], ps[:, T0:T0 + 2, :], ACT.Copy).then_inc(t_act.sem, 1)

                def part(step, i, which):
                    dst, src = parts[i][step[1]], (rr, r1)[which][i]
                    if which == 0:
                        wait(act, qk_st, earlier(step, 2))
                        wait(act, rot_add, step, i + 1)
                    else:
                        wait(act, rest1[i], step)
                    act.activation(dst[:, which], src[:, :, :], ACT.Copy).then_inc((part1, part2)[which].sem, 1)

                def values(step):
                    wait(act, v_st, earlier(step, 1))
                    wait(act, v_pe, step)
                    act.activation(vs[:, :, :, 0:DK].rearrange("p a h v -> p (a h) v"),
                                   ps[:, V0:V0 + 2, :].rearrange("p c (h v) -> p (c h) v", v=DK),
                                   ACT.Copy).then_inc(v_act.sem, 1)

                def gate(step, m):
                    before, mb = slot_user(step, m)
                    wait(act, hid, before, mb + 1)
                    wait(act, gu_pe, step, m + 1)
                    act.activation(sg[:, m % NH], ps[:, FFN[m], :], ACT.Silu, scale=QSCALE).then_inc(silu.sem, 1)

                def high(step, m):
                    if m == 0:
                        wait(act, down_pe, earlier(step, 1))
                    wait(act, hid, step, m + 1)
                    act.activation(hh[:, m], h32[:, m % NH], ACT.Copy).then_inc(hid_hi.sem, 1)

                take_transposed((0, 0))

                def chunk(step, more):
                    part(step, 0, 0)
                    values(step)
                    gate(step, 0)
                    part(step, 1, 0)
                    gate(step, 1)
                    high(step, 0)
                    part(step, 0, 1)
                    gate(step, 2)
                    high(step, 1)
                    part(step, 1, 1)
                    for m in range(3, MH):
                        gate(step, m)
                        high(step, m - 1)
                    high(step, MH - 1)
                    if more:
                        take_transposed(nxt(step))
                    wait(act, g_st, earlier(step, 2))
                    for j in range(2):
                        wait(act, down_pe, step, j + 1)
                        act.activation(gs[:, step[1], 2 * j:2 * j + 2].rearrange("p a d -> p (a d)"), ps[:, V0 + j, :],
                                       ACT.Silu, scale=QSCALE / HSCALE).then_inc(gate_act.sem, 1)

                over_batches(act, chunk)

            @block.tensor
            def _(pe):
                for s in (t_pe, q_pe, k_pe, v_pe, gu_pe, down_pe):
                    s.start(pe)

                def transposes(step):
                    wait(pe, t_lo, earlier(step, 1))
                    wait(pe, ln_xn, step)
                    for kd in range(KD):
                        for a in range(CT):
                            ins = pe.transpose(ps[:, T0 + kd, a * P:(a + 1) * P], xn[:, a, kd * P:(kd + 1) * P], ident[:, :])
                    ins.then_inc(t_pe.sem, 1)

                transposes((0, 0))

                def chunk(step, more):
                    wait(pe, t_act, step)
                    for i, done in enumerate((q_pe, k_pe)):
                        wait(pe, hid, earlier(step, 1), (MH, MH - 1)[i])
                        for eo in range(2):
                            for kd in range(KD):
                                ins = pe.matmul(ps[:, (Q0, K0)[i] + eo, :], wqkT[:, kd, 2 * i + eo, :], xT[:, kd, :],
                                                start=kd == 0, stop=kd == KD - 1)
                        ins.then_inc(done.sem, 1)
                    wait(pe, gate_act, earlier(step, 1))
                    for a in range(CT):
                        for kd in range(KD):
                            ins = pe.matmul(ps[:, V0 + a // 2, (a % 2) * D:(a % 2 + 1) * D], xT[:, kd, a * P:(a + 1) * P],
                                            wvT[:, kd, :], start=kd == 0, stop=kd == KD - 1)
                    ins.then_inc(v_pe.sem, 1)
                    wait(pe, t_lo, step)
                    for m in range(MH):
                        if m < 2:
                            wait(pe, rot_mul, step, m + 1)
                        elif m == 2:
                            wait(pe, v_act, step)
                        else:
                            wait(pe, hid, step, {3: 1, 4: 2, 5: 4}[m])
                        for gu in range(2):
                            n = 0
                            for kd in range(KD):
                                for xx in (xTh, xTl):
                                    ins = pe.matmul(ps[:, FFN[m] + gu, :], wguT[:, gu, kd, m * P:(m + 1) * P],
                                                    xx[:, kd, :], start=n == 0, stop=n == 2 * KD - 1)
                                    n += 1
                        ins.then_inc(gu_pe.sem, 1)
                    if more:
                        transposes(nxt(step))
                    wait(pe, hid, step, 3)

                    def down(a, ms):
                        for m in ms:
                            if a in (0, 2):
                                wait_low(pe, step, m)
                            for n, hx in enumerate((hh, hl)):
                                ins = pe.matmul(ps[:, V0 + a // 2, (a % 2) * D:(a % 2 + 1) * D], hx[:, m, a * P:(a + 1) * P],
                                                wdT[:, m, :], start=m == 0 and n == 0, stop=m == MH - 1 and n == 1)
                        return ins

                    for a in (0, 2):
                        down(a, range(MH - 1))
                    for a in (0, 2):
                        down(a, (MH - 1,))
                    for a in (1, 3):
                        down(a, range(MH)).then_inc(down_pe.sem, 1)

                over_batches(pe, chunk)



def score_units(by_key):
    units = []
    if by_key:
        for c in range(S // CH):
            for kb in range((c + 1) * CT):
                lo = max(kb * P, c * CH)
                w = (c + 1) * CH - lo
                n = min(GH, CH // w)
                units += [(kb, lo, w, tuple(range(h, h + n))) for h in range(0, GH, n)]
    else:
        for qb in range(QB):
            for lo in range(0, (qb + 1) * P, CH):
                w = min(CH, (qb + 1) * P - lo)
                n = 1 << ((CH // w).bit_length() - 1)
                n = min(GH, n)
                units += [(qb, lo, w, tuple(range(h, h + n))) for h in range(0, GH, n)]
    return units


def attention_phase(nc, ps, keep, x, scratch, out):
    q_parts_d, k_parts_d, v_d, gate_d = scratch
    ident, woT = keep["ident"], keep["woT"]
    MAXU, EXPU = score_units(False), score_units(True)
    NU = len(MAXU)
    assert NU == len(EXPU)
    SHIFT = 13
    NSTEP = sum((c + 1) * CT for c in range(S // CH))
    diag_units = [u for u, (kb, lo, w, hs) in enumerate(EXPU) if lo == kb * P]
    ND = len(diag_units)
    ctx = ExitStack()
    with ctx:
        sb = lambda n, s, d: ctx.enter_context(nc.sbuf_tensor(n, s, d))
        sem = lambda n: ctx.enter_context(nc.semaphore(n))
        stage = lambda n, k: Stage(ctx, nc, n, k, NG)

        ROWS = STACK + PARTS
        qs = [sb(f"qs{g}", [P, GH, S], BF16) for g in range(NG)]
        ks = [sb(f"ks{g}", [P, GH, S], BF16) for g in range(NG)]
        vt = [sb(f"vt{i}", [P, QB, GH, VW], F32) for i in range(2)]
        pr = [sb(f"pr{i}", [P, GH, CH], F32) for i in range(3)]
        mxa = [sb(f"mxa{i}", [P, GH, QB], F32) for i in range(2)]
        mxb = [sb(f"mxb{i}", [P, GH, QB // 2], F32) for i in range(2)]
        mneg = sb("mneg", [GH * QB, P], F32)
        mp = sb("mp", [GH * QB, PARTS, P], BF16)
        mr = sb("mr", [GH * QB, P], F32)
        ot = sb("ot", [P, 2, CH], F32)
        rec = sb("rec", [P, 2, CT * GH], F32)
        an = sb("an", [P, QB, D], F32)
        ab = sb("ab", [P, QB, D], F32)
        gt = sb("gt", [P, HALVES, CT, D], F32)
        xt = sb("xt", [P, HALVES, CT, D], F32)
        zt = sb("zt", [P, HALVES, CT, D], F32)
        yt = sb("yt", [P, 2, D], F32)
        aT = sb("aT", [P, 2, KD, P], F32)
        identb = sb("identb", [P, P], BF16)
        future = sb("future", [P, P], BF16)

        s_c = sem("s_c")
        s_held = sem("s_held2")
        s_cl = sem("s_cl")
        qk_ld = [sem(f"qk_ld{g}") for g in range(NG)]
        v_ld = [sem(f"v_ld{g}") for g in range(2)]
        max_pe, max_dve = stage("max_pe", NU), stage("max_dve", NU)
        mx_join, mx_t, mx_neg, mx_parts = stage("mx_join", 1), stage("mx_t", 1), stage("mx_neg", 1), stage("mx_parts", 4)
        mx_ld = stage("mx_ld", 16 * PARTS)
        st_pe, expo, causal = stage("st_pe", NU), stage("expo", NU), stage("causal", ND)
        pv_pe, o_act, o_pe = stage("pv_pe", NSTEP), stage("o_act", 2), stage("o_pe", 2)
        o_rec, o_norm = stage("o_rec", 2), stage("o_norm", 2)
        s_copy = sem("s_copy")
        o_ld = [sem(f"o_ld{c}") for c in range(HALVES)]
        t_tr, t_ev, t_wo, t_mul, t_add = (Stage(ctx, nc, n, 1, QB) for n in ("t_tr", "t_ev", "t_wo", "t_mul", "t_add"))
        o_st = [Stage(ctx, nc, f"o_st{c}", 16, 1) for c in range(HALVES)]

        NST, NMX = 3, 3
        ST0, MX0, O0, M0 = 0, NST, NST + NMX, NST + NMX + 1
        LOADS = 16 * 9

        q_v = q_parts_d.rearrange("b (r h) s -> b r h s", h=H)
        k_v = k_parts_d.rearrange("b (r h) s -> b r h s", h=H)
        halves = lambda d: d.rearrange("b (c a p) d -> b c p a d", c=HALVES, p=P)
        x_v, gate_v, out_v = halves(x), halves(gate_d), halves(out)

        def nth(step, n):
            b, g = step
            d = (g + n) // NG
            return (b + d if d else b), (g + n) % NG

        def before_bank(units_k, step, u, nb):
            lst = [v for v in range(u) if v % nb == u % nb]
            if lst:
                return step, lst[-1] + 1
            lst = [v for v in range(units_k) if v % nb == u % nb]
            return earlier(step, 1), lst[-1] + 1

        with nc.Block() as block:

            def over_groups(eng, group):
                ahead_of = lambda g: lambda n: (B - 1) * NG + g + n < B * NG
                group((0, 0), False, lambda n: True)
                def batch(b):
                    for g in range(1, NG):
                        group((b, g), True, lambda n: True)
                    group((b + 1, 0), True, lambda n: True)
                batch(0)
                with eng.Fori(1, B - 1) as b:
                    batch(b)
                for g in range(1, NG):
                    group((B - 1, g), True, ahead_of(g))

            def output_tiles(step):
                b, g = step
                tiles = ((b - 2, QB - 1), (b - 1, 0)) if g == 0 else ((b - 1, 2 * g - 1), (b - 1, 2 * g))
                return [None if isinstance(t[0], int) and t[0] < 0 else t for t in tiles]

            last_tiles = [(B - 2, QB - 1)] + [(B - 1, t) for t in range(QB)]
            TILE_BANKS = NMX

            def maxima_of(step, ahead):
                out = []
                if ahead(1):
                    out += [(nth(step, 1), u) for u in range(SHIFT, NU)]
                if ahead(2):
                    out += [(nth(step, 2), u) for u in range(SHIFT)]
                return out

            first_maxima = [((0, 0), u) for u in range(NU)] + [((0, 1), u) for u in range(SHIFT)]

            def key_step(u):
                kb, lo, w, hs = EXPU[u]
                c = lo // CH
                return (CT if c else 0) + kb if c else kb

            LAG = 5
            last_of = {}
            for u in range(NU):
                last_of[key_step(u)] = u
            late = [s for s in range(NSTEP) if last_of[s] + LAG >= NU]
            TAKE1 = last_of[NSTEP - 1] + LAG - NU + 1
            OUT1 = TAKE1 + 4
            NORM1 = OUT1 + 2
            TAKE0 = last_of[CT - 1] + LAG + 1
            OUT0 = TAKE0 + 4
            NORM0 = OUT0 + 2
            MAXT = NU - SHIFT + 2
            NEG = MAXT + 1
            TR = (1, 30)
            WO = (4, 33)
            SPLIT_AT = [u for u in diag_units if u > NEG][0]

            def step_before(step, s, n):
                return (step, s - n + 1) if s >= n else (earlier(step, 1), NSTEP + s - n + 1)

            @block.sync
            def _(sp):
                mx_ld.start(sp)
                for s in o_st:
                    s.start(sp)
                sp.wait_ge(s_cl, 1)

                def load_stacks(step):
                    b, g = step
                    h = slice(g * GH, (g + 1) * GH)
                    sp.dma_start(qs[g][0:3 * DK], q_v[b, 0:3 * DK, h]).then_inc(qk_ld[g], 16)
                    sp.dma_start(qs[g][3 * DK:5 * DK], q_v[b, 0:2 * DK, h]).then_inc(qk_ld[g], 16)
                    sp.dma_start(qs[g][5 * DK:6 * DK], q_v[b, 0:DK, h]).then_inc(qk_ld[g], 16)
                    for n, part in enumerate(K_BANDS):
                        sp.dma_start(ks[g][n * DK:(n + 1) * DK], k_v[b, part * DK:(part + 1) * DK, h]).then_inc(qk_ld[g], 16)

                def load_v(step):
                    b, g = step
                    sp.dma_start(vt[g % 2].rearrange("p k h v -> p k (h v)")[:, :, :],
                                 v_d.rearrange("b k p e -> b p k e")[b, :, :, g * GH * VW:(g + 1) * GH * VW]).then_inc(v_ld[g % 2], 16)

                def load_max(step):
                    g = step[1]
                    wait(sp, st_pe, earlier(step, NG))
                    for part in range(PARTS):
                        wait(sp, mx_parts, step, (1, 3, 4)[part])
                        sp.dma_start(qs[g][STACK + part:STACK + part + 1].rearrange("p h (q s) -> p (h q) s", q=QB),
                                     mp[:, part, :]).then_inc(mx_ld.sem, 16)

                for g in range(NG - 1):
                    load_stacks((0, g))
                for g in range(2):
                    load_v((0, g))
                load_max((0, 0))

                def copy_attention(b):
                    wait(sp, o_norm, (b, NG - 1))
                    wait(sp, t_tr, (b - 1, QB - 1))
                    sp.dma_start(ab[:, :, :], an[:, :, :]).then_inc(s_copy, 16)

                def load_output(b, c):
                    wait(sp, t_add, (b - 1, (c + 1) * CT - 1))
                    sp.dma_start(gt[:, c], gate_v[b, c]).then_inc(o_ld[c], 16)
                    sp.dma_start(xt[:, c], x_v[b, c]).then_inc(o_ld[c], 16)

                def store_output(b, c):
                    wait(sp, t_add, (b, (c + 1) * CT - 1))
                    sp.dma_start(out_v[b, c], zt[:, c]).then_inc(o_st[c].sem, 16)

                def group(step, prev, ahead):
                    b, g = step
                    if ahead(3):
                        wait(sp, st_pe, earlier(step, 1))
                        load_stacks(nth(step, 3))
                    if prev:
                        if ahead(1):
                            wait(sp, pv_pe, nth(step, -1))
                            load_v(nth(step, 1))
                    before = output_tiles((b, 1))[0]
                    if g == 0 and prev:
                        copy_attention(b - 1)
                    if g == 1 and before:
                        load_output(b - 1, 1)
                    if g == NG - 1:
                        if before:
                            store_output(b - 1, 0)
                        load_output(b, 0)
                    if ahead(1):
                        load_max(nth(step, 1))
                    if g == 0 and output_tiles(step)[0]:
                        store_output(b - 2, 1)

                over_groups(sp, group)
                store_output(B - 2, 1)
                load_output(B - 1, 1)
                for c in range(HALVES):
                    store_output(B - 1, c)
                for c in range(HALVES):
                    wait(sp, o_st[c], (B - 1, 0))

            @block.gpsimd
            def _(pool):
                for s in (mx_parts, causal, t_add):
                    s.start(pool)
                ch = Chain(pool, s_c)
                ch(pool.memset(identb[:, :], 0.0))
                ch(pool.memset(future[:, :], 0.0))
                ch(pool.affine_select(out=identb[:, :], in_=identb[:, :], compare_op=ALU.not_equal, fill=1.0,
                                      base=0, pattern=[[-1, P]], channel_multiplier=1))
                ch(pool.affine_select(out=future[:, :], in_=future[:, :], compare_op=ALU.is_ge, fill=MASKED,
                                      base=0, pattern=[[-1, P]], channel_multiplier=1))

                def split_max(step):
                    wait(pool, mx_ld, earlier(step, 1))
                    wait(pool, mx_neg, step)
                    hold(pool, s_held)
                    pool.tensor_scalar(mp[:, 0], mneg[:, :], 1.0, 0.0, ALU.mult, ALU.add).then_inc(mx_parts.sem, 1)
                    wait(pool, mx_parts, step, 1)
                    pool.tensor_tensor(mr[:, :], mneg[:, :], mp[:, 0], ALU.subtract).then_inc(mx_parts.sem, 1)
                    wait(pool, mx_parts, step, 2)
                    hold(pool, s_held)
                    pool.tensor_scalar(mp[:, 1], mr[:, :], 1.0, 0.0, ALU.mult, ALU.add).then_inc(mx_parts.sem, 1)
                    wait(pool, mx_parts, step, 3)
                    pool.tensor_tensor(mp[:, 2], mr[:, :], mp[:, 1], ALU.subtract).then_inc(mx_parts.sem, 1)

                def mask(step, n):
                    kb, lo, w, hs = EXPU[diag_units[n]]
                    s = key_step(diag_units[n])
                    blk = pr[s % 3][:, hs[0]:hs[-1] + 1, 0:P]
                    wait(pool, expo, step, diag_units[n] + 1)
                    hold(pool, s_held)
                    pool.affine_select(out=blk, in_=blk, compare_op=ALU.is_ge, fill=0.0, base=0,
                                       pattern=[[0, len(hs)], [1, P]], channel_multiplier=-1).then_inc(causal.sem, 1)

                def add_tile(tile):
                    b, t = tile
                    c = t // CT
                    wait(pool, o_st[c], (b - 1, 0))
                    wait(pool, t_mul, tile)
                    pool.tensor_tensor(zt[:, c, t % CT], yt[:, t % 2], xt[:, c, t % CT], ALU.add).then_inc(t_add.sem, 1)

                split_max((0, 0))

                def group(step, prev, ahead):
                    tiles = output_tiles(step)
                    for n in range(ND):
                        if diag_units[n] == SPLIT_AT and ahead(1):
                            split_max(nth(step, 1))
                        mask(step, n)
                        if diag_units[n] == last_of[CT - 1] and tiles[0]:
                            add_tile(tiles[0])
                    if tiles[1]:
                        add_tile(tiles[1])

                over_groups(pool, group)
                for tile in last_tiles:
                    add_tile(tile)

            def maximum(dve, step, u):
                qb, lo, w, hs = MAXU[u]
                par = step[1] % 2
                dst = mxa[par][:, hs[0]:hs[-1] + 1, qb] if lo == 0 else mxb[par][:, hs[0]:hs[-1] + 1, qb - QB // 2]
                if u == 0:
                    wait(dve, mx_t, earlier(step, 2))
                    wait(dve, mx_join, earlier(step, 2))
                wait(dve, max_pe, step, u + 1)
                dve.tensor_reduce(dst, ps[:, MX0 + u % NMX, 0:w * len(hs)].rearrange("p (h s) -> p h s", s=w),
                                  axis=AX.X, op=ALU.max).then_inc(max_dve.sem, 1)

            def join_max(dve, step):
                par = step[1] % 2
                wait(dve, max_dve, step)
                dve.tensor_tensor(mxa[par][:, :, QB // 2:], mxa[par][:, :, QB // 2:], mxb[par][:, :, :],
                                  ALU.max).then_inc(mx_join.sem, 1)

            def negate_max(dve, step):
                wait(dve, mx_parts, earlier(step, 1))
                wait(dve, mx_t, step)
                dve.tensor_scalar(mneg[:, :], ps[0:GH * QB, M0, 0:P], -1.0, None, ALU.mult).then_inc(mx_neg.sem, 1)

            @block.vector
            def _(dve):
                for s in (max_dve, mx_join, mx_neg, o_rec, o_norm, t_mul):
                    s.start(dve)
                for g in range(NG):
                    ins = dve.memset(ks[g][STACK:ROWS].bitcast(F32), ONES_TWICE)
                ins.then_inc(s_cl, 1)

                def normalise(step, c):
                    o = ps[:, M0, :].rearrange("p (r v) -> p r v", v=VW)
                    b, g = step
                    if g == 0 and c == 0 and output_tiles((b, 1))[0]:
                        dve.wait_ge(s_copy, b * 16)
                    wait(dve, o_norm, earlier(step, 1), c + 1)
                    wait(dve, o_pe, step, c + 1)
                    dve.reciprocal(rec[:, c], o[:, :, DK]).then_inc(o_rec.sem, 1)
                    wait(dve, o_rec, step, c + 1)
                    dve.tensor_tensor(an[:, c * CT:(c + 1) * CT, g * GH * DK:(g + 1) * GH * DK].rearrange("p q (h e) -> p q h e", e=DK),
                                      o[:, :, 0:DK].rearrange("p (q h) e -> p q h e", h=GH),
                                      rec[:, c].rearrange("p (q h) -> p q h", h=GH).unsqueeze(3).to_broadcast([P, CT, GH, DK]),
                                      ALU.mult).then_inc(o_norm.sem, 1)

                def gate_tile(tile, bank):
                    b, t = tile
                    c = t // CT
                    if t % CT == 0:
                        dve.wait_ge(o_ld[c], b * 32 + 32)
                    wait(dve, t_add, earlier(tile, 2))
                    wait(dve, t_wo, tile)
                    dve.tensor_tensor(yt[:, t % 2], ps[:, bank, D:2 * D], gt[:, c, t % CT], ALU.mult).then_inc(t_mul.sem, 1)

                for ms, u in first_maxima:
                    maximum(dve, ms, u)
                    if (ms, u) == ((0, 0), NU - 1):
                        join_max(dve, ms)
                        negate_max(dve, ms)

                def group(step, prev, ahead):
                    todo = maxima_of(step, ahead)
                    tiles = output_tiles(step)
                    for n in range(NU):
                        if n < len(todo):
                            ms, u = todo[n]
                            maximum(dve, ms, u)
                            if u == NU - 1:
                                join_max(dve, ms)
                        if n == NORM1 and prev:
                            normalise(nth(step, -1), 1)
                        if n == NORM0:
                            normalise(step, 0)
                        if n == NEG and ahead(1):
                            negate_max(dve, nth(step, 1))
                        for i in range(2):
                            if n == WO[i] + 1 and tiles[i]:
                                gate_tile(tiles[i], M0)

                over_groups(dve, group)
                normalise((B - 1, NG - 1), 1)
                for i, tile in enumerate(last_tiles):
                    gate_tile(tile, MX0 + i % TILE_BANKS)

            @block.scalar
            def _(act):
                for s in (expo, o_act, t_ev):
                    s.start(act)

                def exponentials(step, u):
                    kb, lo, w, hs = EXPU[u]
                    s = key_step(u)
                    prev = step_before(step, s, 3)
                    wait(act, pv_pe, *prev)
                    wait(act, st_pe, step, u + 1)
                    act.activation(pr[s % 3][:, hs[0]:hs[-1] + 1, 0:w],
                                   ps[:, ST0 + u % NST, 0:w * len(hs)].rearrange("p (h s) -> p h s", s=w),
                                   ACT.Exp, scale=1.0 / DK ** 0.5).then_inc(expo.sem, 1)

                def take_output(step, c):
                    wait(act, o_pe, earlier(step, 1), c + 1)
                    wait(act, pv_pe, step, CT if c == 0 else NSTEP)
                    act.activation(ot[:, c], ps[:, O0, :], ACT.Copy).then_inc(o_act.sem, 1)

                def take_tile(tile, bank):
                    wait(act, t_wo, earlier(tile, 2))
                    wait(act, t_tr, tile)
                    act.activation(aT[:, tile[1] % 2], ps[:, bank, 0:D].rearrange("p (k t) -> p k t", k=KD),
                                   ACT.Copy).then_inc(t_ev.sem, 1)

                def group(step, prev, ahead):
                    tiles = output_tiles(step)
                    for u in range(NU):
                        exponentials(step, u)
                        for i in range(2):
                            if u == TR[i] + 1 and tiles[i]:
                                take_tile(tiles[i], M0)
                        if u == TAKE1 and prev:
                            take_output(nth(step, -1), 1)
                        if u == TAKE0:
                            take_output(step, 0)

                over_groups(act, group)
                take_output((B - 1, NG - 1), 1)
                for i, tile in enumerate(last_tiles):
                    take_tile(tile, MX0 + i % TILE_BANKS)

            @block.tensor
            def _(pe):
                for s in (max_pe, mx_t, st_pe, pv_pe, o_pe, t_tr, t_wo):
                    s.start(pe)
                pe.wait_ge(s_c, 4)
                pe.wait_ge(s_cl, 1)

                def queries_by_keys(step, u):
                    qb, lo, w, hs = MAXU[u]
                    b, g = step
                    if u == 0:
                        pe.wait_ge(qk_ld[g], b * LOADS + LOADS)
                    wait(pe, max_dve, *before_bank(NU, step, u, NMX))
                    diag = lo + w > qb * P
                    for n, h in enumerate(hs):
                        o = ps[:, MX0 + u % NMX, n * w:(n + 1) * w]
                        ins = pe.matmul(o, qs[g][0:STACK, h, qb * P:(qb + 1) * P], ks[g][0:STACK, h, lo:lo + w],
                                        start=n == 0, stop=not diag, skip_group_check=True)
                        if diag:
                            ins = pe.matmul(o[:, w - P:w], identb[:, :], future[:, :], start=False, stop=True,
                                            skip_group_check=True)
                    ins.then_inc(max_pe.sem, 1)

                def keys_by_queries(step, u):
                    kb, lo, w, hs = EXPU[u]
                    g = step[1]
                    if u == 0:
                        wait(pe, mx_ld, step)
                    wait(pe, expo, *before_bank(NU, step, u, NST))
                    for n, h in enumerate(hs):
                        ins = pe.matmul(ps[:, ST0 + u % NST, n * w:(n + 1) * w], ks[g][0:ROWS, h, kb * P:(kb + 1) * P],
                                        qs[g][0:ROWS, h, lo:lo + w], start=True, stop=True)
                    ins.then_inc(st_pe.sem, 1)

                def times_v(step, s):
                    b, g = step
                    c = 0 if s < CT else 1
                    kb = s if s < CT else s - CT
                    lo = max(kb * P - c * CH, 0)
                    if s == 0:
                        pe.wait_ge(v_ld[g % 2], b * 32 + 16 * (g // 2) + 16)
                    if kb == 0:
                        wait(pe, o_act, *((step, 1) if c else (earlier(step, 1), 2)))
                    nd = [n for n, u in enumerate(diag_units) if key_step(u) == s]
                    if nd:
                        wait(pe, causal, step, nd[-1] + 1)
                    wait(pe, expo, step, last_of[s] + 1)
                    for j in range(GH):
                        ins = pe.matmul(ps[VW * j:VW * (j + 1), O0, lo:CH], vt[g % 2][:, kb, j, :],
                                        pr[s % 3][:, j, 0:CH - lo], start=kb == 0, stop=kb == (c + 1) * CT - 1)
                    ins.then_inc(pv_pe.sem, 1)

                def transpose_max(step):
                    wait(pe, o_norm, earlier(step, 1), 1)
                    wait(pe, mx_join, step)
                    pe.matmul(ps[0:GH * QB, M0, 0:P], mxa[step[1] % 2].rearrange("p h q -> p (h q)")[:, :], ident[:, :],
                              start=True, stop=True).then_inc(mx_t.sem, 1)

                def transpose_output(step, c, tile=None):
                    if c == 0:
                        wait(pe, o_norm, earlier(step, 1))
                    elif tile:
                        wait(pe, t_mul, tile)
                    else:
                        wait(pe, mx_neg, nth(step, 1))
                    wait(pe, o_norm, step, c)
                    wait(pe, o_act, step, c + 1)
                    for a in range(CT):
                        ins = pe.transpose(ps[:, M0, a * P:(a + 1) * P], ot[:, c, a * P:(a + 1) * P], ident[:, :])
                    ins.then_inc(o_pe.sem, 1)

                def transpose_tile(tile, bank, source):
                    t = tile[1]
                    for kd in range(KD):
                        ins = pe.transpose(ps[:, bank, kd * P:(kd + 1) * P], source[:, t, kd * P:(kd + 1) * P], ident[:, :])
                    ins.then_inc(t_tr.sem, 1)

                def project_tile(tile, bank):
                    wait(pe, t_ev, tile)
                    for kd in range(KD):
                        ins = pe.matmul(ps[:, bank, D:2 * D], aT[:, tile[1] % 2, kd, :], woT[:, kd, :],
                                        start=kd == 0, stop=kd == KD - 1)
                    ins.then_inc(t_wo.sem, 1)

                for ms, u in first_maxima:
                    queries_by_keys(ms, u)
                    if (ms, u) == ((0, 0), NU - 1):
                        transpose_max((0, 0))

                def group(step, prev, ahead):
                    todo = maxima_of(step, ahead)
                    tiles = output_tiles(step)
                    for n in range(NU):
                        keys_by_queries(step, n)
                        if n < len(todo):
                            queries_by_keys(*todo[n])
                        for s in range(NSTEP):
                            if last_of[s] + LAG == n:
                                times_v(step, s)
                            if prev and last_of[s] + LAG == n + NU:
                                times_v(nth(step, -1), s)
                        if n == TR[0] and tiles[0]:
                            wait(pe, t_mul, earlier(tiles[0], 1))
                            transpose_tile(tiles[0], M0, ab)
                        if n == TR[1] and tiles[1]:
                            if ahead(1):
                                wait(pe, mx_neg, nth(step, 1))
                            else:
                                wait(pe, o_norm, step, 1)
                            if tiles[1][1] == 0:
                                pe.wait_ge(s_copy, (tiles[1][0] + 1) * 16)
                            transpose_tile(tiles[1], M0, ab)
                        for i in range(2):
                            if n == WO[i] and tiles[i]:
                                project_tile(tiles[i], M0)
                        if n == OUT1 and prev:
                            transpose_output(nth(step, -1), 1, tiles[0])
                        if n == OUT0:
                            transpose_output(step, 0)
                        if n == MAXT and ahead(1):
                            transpose_max(nth(step, 1))

                over_groups(pe, group)
                for s in late:
                    times_v((B - 1, NG - 1), s)

                def next_tile(i):
                    b, t = last_tiles[i]
                    bank = MX0 + i % TILE_BANKS
                    if i >= TILE_BANKS:
                        wait(pe, t_mul, last_tiles[i - TILE_BANKS])
                    if b == B - 1:
                        wait(pe, o_norm, (B - 1, NG - 1), t // CT + 1)
                    transpose_tile((b, t), bank, ab if b < B - 1 else an)

                wait(pe, max_dve, (B - 1, NG - 1))
                next_tile(0)
                transpose_output((B - 1, NG - 1), 1, output_tiles((B - 1, NG - 1))[1])
                for i in range(len(last_tiles)):
                    if i + 1 < len(last_tiles):
                        next_tile(i + 1)
                    project_tile(last_tiles[i], MX0 + i % TILE_BANKS)


def program(nc, x, wq, wk, wv, wo, w_gate, w_up, w_down, cs, out):
    nc.disable_value_cache = True
    q_parts_d = nc.dram_tensor("q_parts_d", [B, PARTS * 2 * P, S], BF16).ap()
    k_parts_d = nc.dram_tensor("k_parts_d", [B, PARTS * 2 * P, S], BF16).ap()
    v_d = nc.dram_tensor("v_d", [B, QB, P, H * VW], F32).ap()
    gate_d = nc.dram_tensor("gate_d", [B, S, D], F32).ap()
    with ExitStack() as ctx:
        ps = ctx.enter_context(nc.psum_tensor("ps", [P, 8, 512], F32))
        keep = {"ident": ctx.enter_context(nc.sbuf_tensor("ident", [P, P], F32)),
                "woT": ctx.enter_context(nc.sbuf_tensor("woT", [P, KD, D], F32))}
        project_phase(nc, ps, keep, x, wq, wk, wv, wo, w_gate, w_up, w_down, cs, (q_parts_d, k_parts_d, v_d, gate_d))
        attention_phase(nc, ps, keep, x, (q_parts_d, k_parts_d, v_d, gate_d), out)


_INS = ["L0_attn_x", "L0_attn_wq", "L0_attn_wk", "L0_attn_wv", "L0_attn_wo", "L0_ffn_w_gate", "L0_ffn_w_up", "L0_ffn_w_down"]


def kernel(**inputs):
    import numpy as _np
    import concourse.bacc as _bacc
    from concourse import mybir as _mybir
    from concourse.bass_utils import run_bass_kernel_spmd as _run

    nc = _bacc.Bacc("TRN2", target_bir_lowering=False, num_devices=1)
    arrays, args = {}, []
    for name in _INS:
        a = _np.ascontiguousarray(inputs[name])
        arrays[f"in_{name}"] = a
        args.append(nc.dram_tensor(f"in_{name}", a.shape, _mybir.dt.from_np(a.dtype), kind="ExternalInput").ap())
    f = _np.float32
    angle = _np.arange(S, dtype=f)[:, None] / f(10000.0) ** (f(2.0) * _np.arange(PAIRS, dtype=f)[None, :] / f(DK))
    sin, cos = (_np.repeat(t(angle).T, H, axis=0) for t in (_np.sin, _np.cos))
    a = _np.ascontiguousarray(_np.stack([_np.stack([cos, -sin], 1), _np.stack([sin, cos], 1)], 1))
    arrays["in_trig"] = a
    args.append(nc.dram_tensor("in_trig", a.shape, F32, kind="ExternalInput").ap())
    args.append(nc.dram_tensor("out_dram", (B, S, D), F32, kind="ExternalOutput").ap())
    program(nc, *args)
    r = _run(nc, [arrays], core_ids=[0])
    return r.results[0]["out_dram"]
```

```python
import concourse.bass as bass
from concourse import mybir
from contextlib import ExitStack

F32 = mybir.dt.float32
F16 = mybir.dt.float16
BF16 = mybir.dt.bfloat16
I32 = mybir.dt.int32
ACT = mybir.ActivationFunctionType
ALU = mybir.AluOpType
AX = mybir.AxisListType

P = 128
B, S, D = 8, 1024, 256
H, DK = 16, 16
HID = 768
EPS = 1e-5
QSCALE = 1.0 / 127.0
HSCALE = 0.125
KD = D // P
MH = HID // P
CH = 512
CT = CH // P
HALVES = S // CH
PAIRS = DK // 2
GH = 4
NG = H // GH
QB = S // P
VW = 32
PARTS = 3
STACK = 6 * DK
MASKED = -3.0e38
EXP_BITS = 0x7F800000
TARGET = 6
LEAST = 32
ONES_TWICE = 1.0 + 0x3F80 * 2.0 ** -23
Q_BANDS = (0, 1, 2, 0, 1, 0)
K_BANDS = (0, 0, 0, 1, 1, 2)


class Stage:

    def __init__(self, ctx, nc, name, k, per):
        self.sem = ctx.enter_context(nc.semaphore(name))
        self.k, self.per = k, per
        self.lead = per + 2

    def start(self, eng):
        eng.sem_inc(self.sem, self.lead * self.k)

    def after(self, step, count=None):
        loop, off = step
        count = self.k if count is None else count
        return loop * (self.per * self.k) + ((off + self.lead) * self.k + count)


def wait(eng, stage, step, count=None):
    eng.wait_ge(stage.sem, stage.after(step, count))


def hold(eng, sem):
    eng.sem_inc(sem, 1)


def earlier(step, n):
    return step[0], step[1] - n


class Chain:

    def __init__(self, eng, sem):
        self.eng, self.sem, self.n = eng, sem, 0

    def __call__(self, instruction):
        instruction.then_inc(self.sem, 1)
        self.n += 1
        self.eng.wait_ge(self.sem, self.n)


def project_phase(nc, ps, keep, x, wq, wk, wv, wo, w_gate, w_up, w_down, cs, scratch):
    q_parts_d, k_parts_d, v_d, gate_d = scratch
    ident, woT, gs, g_st = keep["ident"], keep["woT"], keep["gs"], keep["g_st"]
    ctx = ExitStack()
    with ctx:
        sb = lambda n, s, d: ctx.enter_context(nc.sbuf_tensor(n, s, d))
        sem = lambda n: ctx.enter_context(nc.semaphore(n))
        stage = lambda n, k: Stage(ctx, nc, n, k, HALVES)

        wqkT = sb("wqkT", [P, 2, KD, 4, P], F16)
        wvT = sb("wvT", [P, 2, KD, D], F16)
        winv = sb("winv", [P, 4], F32)
        wguT = sb("wguT", [P, 2, KD, HID], F16)
        wdT = sb("wdT", [P, MH, D], F16)
        trig = sb("trig", [P, 2, 2, S], F32)
        table = sb("table1", [1, 1], F32)
        negh = sb("negh", [P, CT], F32)

        xs = sb("xs", [P, 2, CT, D], F32)
        st = sb("st", [P, CT, 6], F32)
        mv = sb("mv", [P, CT, 2], F32)
        ve = sb("ve", [P, CT], F32)
        rstd = sb("rstd", [P, CT], F32)
        xn = sb("xn", [P, CT, D], F32)
        xh = sb("xh", [P, CT, D], F16)
        xl = sb("xl", [P, CT, D], F16)
        identh = sb("identh", [P, P], F16)
        xTh = sb("xTh", [P, KD, CH], F16)
        xTl = sb("xTl", [P, KD, CH], F16)
        vs = sb("vs", [P, CT, H, VW], F32)

        s_const = sem("s_const")
        s_one = sem("s_one")
        s_max, s_maxT, s_scale, s_low = sem("s_max"), sem("s_maxT"), sem("s_scale"), sem("s_low")
        s_held = sem("s_held")
        s_wload = sem("s_wload")
        s_iload = [sem(f"s_iload{i}") for i in range(3)]
        s_prep = sem("s_prep")
        s_wt = sem("s_wt")
        s_we = [sem(f"s_we{i}") for i in range(2)]
        x_ld = [stage(f"x_ld{i}", 0) for i in range(2)]
        ln_stat, ln_aggr = stage("ln_stat", 1), stage("ln_aggr", 1)
        ln_ve, ln_rs, ln_xn = stage("ln_ve", 1), stage("ln_rs", 1), stage("ln_xn", 1)
        x_hi, x_lo = stage("x_hi", 1), stage("x_lo", 1)
        t_pe, t_hi, t_lo = stage("t_pe", 1), stage("t_hi", 1), stage("t_lo", 1)
        q_pe, k_pe, v_pe = stage("q_pe", 1), stage("k_pe", 1), stage("v_pe", 1)
        rot_mul, rot_add = stage("rot_mul", 2), stage("rot_add", 2)
        part1, part2, part3 = stage("part1", 2), stage("part2", 2), stage("part3", 2)
        rest1 = stage("rest1q", 1), stage("rest1k", 1)
        v_act = stage("v_act", 1)
        gu_pe, silu, hid = stage("gu_pe", MH), stage("silu", MH), stage("hid", MH)
        LOW_POOL = 4
        hid_hi = stage("hid_hi", MH)
        lo_pool, lo_dve = stage("lo_pool", LOW_POOL), stage("lo_dve", MH - LOW_POOL)
        down_pe, gate_act = stage("down_pe", 2), stage("gate_act", 2)
        qk_st, v_st = stage("qk_st", 32), stage("v_st", 16)

        T0, Q0, K0, V0 = 0, 2, 4, 6
        FFN = (Q0, K0, V0, Q0, K0, Q0)

        x_v = x.rearrange("b (c a p) d -> b c p a d", c=HALVES, p=P)

        def x_arrived(eng, step):
            b, c = step
            if c >= HALVES:
                b, c = b + 1, c - HALVES
            eng.wait_ge(x_ld[c].sem, b * 16 + 16)
            return c

        def stats(dve, step):
            c = x_arrived(dve, step)
            wait(dve, ln_aggr, earlier(step, 1))
            for a in range(CT):
                ins = dve.bn_stats(st[:, a], xs[:, c, a])
            ins.then_inc(ln_stat.sem, 1)
            wait(dve, ln_rs, earlier(step, 1))
            wait(dve, ln_xn, earlier(step, 1))
            wait(dve, ln_stat, step)
            hold(dve, s_held)
            for a in range(CT):
                ins = dve.bn_aggr(mv[:, a], st[:, a])
            ins.then_inc(ln_aggr.sem, 1)

        def normalise(dve, step):
            c = step[1] % HALVES
            wait(dve, x_hi, earlier(step, 1))
            wait(dve, x_lo, earlier(step, 1))
            wait(dve, ln_rs, step)
            for a in range(CT):
                ins = dve.tensor_scalar(xn[:, a], xs[:, c, a], mv[:, a, 0:1], rstd[:, a:a + 1],
                                        ALU.subtract, ALU.mult)
            ins.then_inc(ln_xn.sem, 1)

        def inverse_root(pool, step):
            wait(pool, ln_xn, earlier(step, 1))
            wait(pool, ln_aggr, step)
            hold(pool, s_held)
            pool.tensor_scalar(ve[:, :], mv[:, :, 1], EPS, 1.0, ALU.add, ALU.mult).then_inc(ln_ve.sem, 1)
            wait(pool, ln_ve, step)
            pool.tensor_tensor(rstd[:, :], ve[:, :], negh[:, :], ALU.pow).then_inc(ln_rs.sem, 1)

        def high_tokens(act, step):
            wait(act, t_pe, earlier(step, 1))
            wait(act, ln_xn, step)
            act.activation(xh[:, :, :], xn[:, :, :], ACT.Copy).then_inc(x_hi.sem, 1)

        def low_tokens(pool, step):
            wait(pool, t_pe, earlier(step, 1))
            wait(pool, x_hi, step)
            pool.tensor_tensor(xl[:, :, :], xn[:, :, :], xh[:, :, :], ALU.subtract).then_inc(x_lo.sem, 1)

        with ExitStack() as pre, nc.Block() as block:
            raw = pre.enter_context(nc.sbuf_tensor("raw", [P, 8, D], F32))
            rawi = pre.enter_context(nc.sbuf_tensor("rawi", [P, 18, D], I32))
            rawf = pre.enter_context(nc.sbuf_tensor("rawf", [P, 18, D], F32))
            wmax = pre.enter_context(nc.sbuf_tensor("wmax", [P, 4], F32))
            wmaxT = pre.enter_context(nc.sbuf_tensor("wmaxT", [4, 1], F32))
            ones4 = pre.enter_context(nc.sbuf_tensor("ones4", [4, P], F32))
            diag4 = pre.enter_context(nc.sbuf_tensor("diag4", [4, 4], F32))
            wbits = pre.enter_context(nc.sbuf_tensor("wbits", [P, 4], I32))
            wscale = pre.enter_context(nc.sbuf_tensor("wscale", [P, 4], F32))
            SCALE_STEPS = 7

            @block.sync
            def _(sp):
                for i, w in enumerate((wq, wk, wv, wo)):
                    sp.dma_start(raw[:, 2 * i:2 * i + 2, :], w.rearrange("(m p) d -> p m d", p=P)).then_inc(s_wload, 16)
                sp.dma_start(xs[:, 0], x_v[0, 0]).then_inc(x_ld[0].sem, 16)
                for i, w in enumerate((w_gate, w_up)):
                    sp.dma_start(rawi[:, 6 * i:6 * i + 6, :], w.rearrange("(m p) d -> p m d", p=P)).then_inc(s_iload[i], 16)
                sp.dma_start(rawi[:, 12:18, :].rearrange("p (a m) e -> p a (m e)", a=2),
                             w_down.rearrange("(a p) e -> p a e", p=P)).then_inc(s_iload[2], 16)
                sp.dma_start(xs[:, 1], x_v[0, 1]).then_inc(x_ld[1].sem, 16)
                sp.dma_start(trig[:, :, :, :], cs[:, :, :, :]).then_inc(s_const, 16)

            @block.gpsimd
            def _(pool):
                for s in (ln_ve, ln_rs, x_lo):
                    s.start(pool)
                ch = Chain(pool, s_prep)
                ch(pool.memset(ident[:, :], 0.0))
                ch(pool.affine_select(out=ident[:, :], in_=ident[:, :], compare_op=ALU.not_equal, fill=1.0,
                                      base=0, pattern=[[-1, P]], channel_multiplier=1))
                ch(pool.memset(ones4[:, :], 1.0))
                ch(pool.memset(identh[:, :], 0.0))
                ch(pool.affine_select(out=identh[:, :], in_=identh[:, :], compare_op=ALU.not_equal, fill=1.0,
                                      base=0, pattern=[[-1, P]], channel_multiplier=1))
                ch(pool.memset(negh[:, :], -0.5))
                ch(pool.memset(table[:, :], 0.0))
                ch(pool.memset(vs[:, :, :, :], 0.0))
                ch(pool.memset(vs[:, :, :, DK:DK + 1], 1.0))
                pool.wait_ge(s_scale, SCALE_STEPS)
                ones = vs[:, :, :, DK]
                ch(pool.tensor_tensor(ones, ones, wscale[:, 2:3].unsqueeze(2).to_broadcast([P, CT, H]), ALU.mult))
                inverse_root(pool, (0, 0))
                low_tokens(pool, (0, 0))

            banks = []
            split = []
            for i in range(4):
                srcs = [raw[:, 2 * i + m, kd * P:(kd + 1) * P] for kd in range(KD) for m in range(2)]
                flat = lambda t: t.rearrange("p k e -> p (k e)")
                banks.append((srcs, [(flat(woT[:, :, :]), None, None)] if i == 3 else []))
                if i < 2:
                    split.append([([wqkT[:, hl, kd, 2 * i + eo, :].rearrange("p (i h) -> p i h", h=H) for hl in range(2)], kd, eo)
                                  for kd in range(KD) for eo in range(2)])
                elif i == 2:
                    split.append([([flat(wvT[:, hl]) for hl in range(2)], None, None)])
            n_float = len(banks)
            for gu in range(2):
                for kd in range(KD):
                    for m in range(0, MH, 2):
                        banks.append(([rawf[:, 6 * gu + mm, kd * P:(kd + 1) * P] for mm in (m, m + 1)],
                                      [(wguT[:, gu, kd, m * P:(m + 2) * P], None, None)]))
            down = rawf[:, 12:18, :].rearrange("p (a m) e -> p a (m e)", a=2)
            for m in range(0, MH, 2):
                banks.append(([down[:, a, mm * P:(mm + 1) * P] for mm in (m, m + 1) for a in range(2)],
                              [(wdT[:, m:m + 2, :].rearrange("p m d -> p (m d)"), None, None)]))

            by_dve = [0, 1, 2] + list(range(n_float, len(banks), 2))
            by_act = [n for n in range(len(banks)) if n not in by_dve]

            def source_of(n, kd, eo):
                if kd is None:
                    return ps[:, n % 8, 0:P * len(banks[n][0])]
                return ps[:, n % 8, kd * D:(kd + 1) * D].rearrange("p (h i two) -> p two i h", i=PAIRS, two=2)[:, eo]

            def evacuate(eng, copy, n):
                eng.wait_ge(s_wt, n + 1)
                for dst, kd, eo in banks[n][1]:
                    ins = copy(dst, source_of(n, kd, eo))
                ins.then_inc(s_we[0 if n in by_dve else 1], 1)

            @block.vector
            def _(dve):
                for s in (ln_stat, ln_aggr, ln_xn):
                    s.start(dve)
                dve.wait_ge(s_wload, 16 * 4)
                dve.tensor_reduce(wmax[:, :], raw.rearrange("p (w m) d -> p w (m d)", m=2)[:, :, :], axis=AX.X,
                                  op=ALU.max, apply_absolute_value=True).then_inc(s_max, 1)
                stats(dve, (0, 0))
                ch = Chain(dve, s_scale)
                dve.wait_ge(s_maxT, 1)
                ch(dve.tensor_reduce(wmaxT[:, :], ps[0:4, 7, 0:P], axis=AX.X, op=ALU.max))
                ch(dve.tensor_tensor(diag4[:, :], ident[0:4, 0:4], wmaxT[:, :].to_broadcast([4, 4]), ALU.mult))
                dve.wait_ge(s_maxT, 2)
                ch(dve.tensor_copy(wscale[:, :], ps[:, 7, P:P + 4]))
                ch(dve.tensor_scalar(wbits[:, :], wscale[:, :].bitcast(I32), EXP_BITS, None, ALU.bitwise_and))
                ch(dve.tensor_scalar(wbits[:, :], wbits[:, :], float(LEAST << 23), None, ALU.max))
                ch(dve.tensor_scalar(wscale[:, :].bitcast(I32), wbits[:, :], -1.0, float((254 + TARGET) << 23), ALU.mult, ALU.add))
                ch(dve.tensor_scalar(winv[:, :].bitcast(I32), wbits[:, :], 1.0, float(-(TARGET << 23)), ALU.mult, ALU.add))
                assert ch.n == SCALE_STEPS
                for n in range(3):
                    dve.wait_ge(s_iload[n], 16)
                    dve.tensor_copy(rawf[:, 6 * n:6 * n + 6], rawi[:, 6 * n:6 * n + 6]).then_inc(s_one, 1)
                    dve.wait_ge(s_low, n + 1)
                    for (hi, lo), kd, eo in split[n]:
                        ins = dve.scalar_tensor_tensor(out=lo, in0=source_of(n, kd, eo), scalar=wscale[:, n:n + 1], in1=hi,
                                                       op0=ALU.mult, op1=ALU.subtract)
                    ins.then_inc(s_we[0], 1)
                normalise(dve, (0, 0))
                for n in by_dve[3:]:
                    evacuate(dve, dve.tensor_copy, n)

            @block.scalar
            def _(act):
                x_hi.start(act)
                act.wait_ge(s_prep, 7)
                act.activation(table[:, :], table[:, :], ACT.Copy).then_inc(s_held, 1)
                act.wait_ge(s_scale, SCALE_STEPS)
                for n in range(3):
                    act.wait_ge(s_wt, n + 1)
                    for (hi, lo), kd, eo in split[n]:
                        ins = act.activation(hi, source_of(n, kd, eo), ACT.Copy, scale=wscale[:, n:n + 1])
                    ins.then_inc(s_low, 1)
                for n in by_act:
                    if n == 9:
                        high_tokens(act, (0, 0))
                    evacuate(act, lambda dst, src: act.activation(dst, src, ACT.Copy), n)

            @block.tensor
            def _(pe):
                pe.wait_ge(s_prep, 2)
                t_pe.start(pe)
                pe.wait_ge(s_prep, 3)
                pe.wait_ge(s_max, 1)
                pe.transpose(ps[0:4, 7, 0:P], wmax[:, :], ident[:, :]).then_inc(s_maxT, 1)
                pe.wait_ge(s_scale, 2)
                pe.matmul(ps[:, 7, P:P + 4], ones4[:, :], diag4[:, :], start=True, stop=True).then_inc(s_maxT, 1)
                pe.wait_ge(s_wload, 16 * 4)
                for n, (srcs, _) in enumerate(banks):
                    if n >= n_float:
                        pe.wait_ge(s_one, 1 + (n - n_float) // MH)
                    if n == 7:
                        pe.wait_ge(s_scale, 3)
                    if n >= 8:
                        m = n - 8
                        if m in by_dve:
                            pe.wait_ge(s_we[0], by_dve.index(m) + 1)
                        else:
                            pe.wait_ge(s_we[1], by_act.index(m) + 1)
                    for j, src in enumerate(srcs):
                        ins = pe.transpose(ps[:, n % 8, j * P:(j + 1) * P], src, ident[:, :])
                    ins.then_inc(s_wt, 1)

        tq = [sb(f"rot{i}", [P, 2, 2, CH], F32) for i in range(2)]
        rr = [sb(f"rr{i}", [P, 2, CH], F32) for i in range(2)]
        r1 = [sb(f"r1{i}", [P, 2, CH], F32) for i in range(2)]
        parts = [[sb(f"parts{i}{j}", [P, PARTS, 2, CH], BF16) for j in range(2)] for i in range(2)]
        NH = 4
        sg = sb("sg", [P, NH, CH], F32)
        h32 = sb("h32", [P, NH, CH], F32)
        hh = sb("hh", [P, MH, CH], F16)
        hl = sb("hl", [P, MH, CH], F16)

        qk_dst = [d.rearrange("b (r p) s -> b p r s", p=P) for d in (q_parts_d, k_parts_d)]
        gate_v = gate_d.rearrange("b (c a p) d -> b c p a d", c=HALVES, p=P)
        v_v = v_d.rearrange("b (c a) p e -> b c p a e", c=HALVES)

        with nc.Block() as block:

            def over_batches(eng, chunk):
                with eng.Fori(0, B - 1) as b:
                    for c in range(HALVES):
                        chunk((b, c), True)
                for c in range(HALVES):
                    chunk((B - 1, c), c + 1 < HALVES)

            @block.sync
            def _(sp):
                for s in (qk_st, v_st, g_st):
                    s.start(sp)
                def chunk(step, more):
                    b, c = step
                    if not isinstance(b, int):
                        wait(sp, ln_xn, step)
                        sp.dma_start(xs[:, c], x_v[b + 1, c]).then_inc(x_ld[c].sem, 16)
                    for i in range(2):
                        wait(sp, part3, step, i + 1)
                        sp.dma_start(qk_dst[i][b, :, :, c * CH:(c + 1) * CH],
                                     parts[i][c].rearrange("p a e s -> p (a e) s")[:, :, :]).then_inc(qk_st.sem, 16)
                    wait(sp, v_act, step)
                    sp.dma_start(v_v[b, c], vs.rearrange("p a h v -> p a (h v)")[:, :, :]).then_inc(v_st.sem, 16)
                    if not more:
                        wait(sp, qk_st, (B - 2, HALVES - 1))
                        load_stacks(sp, keep, (q_parts_d, k_parts_d), (0, 0))
                    wait(sp, gate_act, step)
                    sp.dma_start(gate_v[b, c], gs[:, c]).then_inc(g_st.sem, 16)

                over_batches(sp, chunk)
                for s in (qk_st, v_st):
                    wait(sp, s, (B - 1, HALVES - 1))

            def slot_user(step, m):
                return (step, m - NH) if m >= NH else (earlier(step, 1), MH + m - NH)

            def wait_low(eng, step, m):
                if m < LOW_POOL:
                    wait(eng, lo_pool, step, m + 1)
                else:
                    wait(eng, lo_dve, step, m - LOW_POOL + 1)

            def rest(eng, step, i):
                wait(eng, part2, earlier(step, 1), i + 1)
                wait(eng, part3, earlier(step, 1), i + 1)
                wait(eng, rot_add, step, i + 1)
                wait(eng, part1, step, i + 1)
                eng.tensor_tensor(r1[i][:, :, :], rr[i][:, :, :], parts[i][step[1]][:, 0], ALU.subtract).then_inc(rest1[i].sem, 1)

            def low(eng, step, m):
                if m in (0, LOW_POOL):
                    wait(eng, down_pe, earlier(step, 1))
                wait(eng, hid_hi, step, m + 1)
                eng.tensor_tensor(hl[:, m], h32[:, m % NH], hh[:, m], ALU.subtract).then_inc((lo_pool if m < LOW_POOL else lo_dve).sem, 1)

            def nxt(step):
                return step[0], step[1] + 1

            @block.vector
            def _(dve):
                for s in (t_lo, rot_mul, part3, hid, rest1[0], lo_dve):
                    s.start(dve)

                def take_low(step):
                    wait(dve, t_pe, step)
                    dve.tensor_copy(xTl.rearrange("p k s -> p (k s)")[:, :], ps[:, T0 + 1, :].bitcast(F16)).then_inc(t_lo.sem, 1)

                dve.wait_ge(s_const, 16)

                def rotate(step, i, pe_stage):
                    c = step[1]
                    wait(dve, rot_add, earlier(step, 1), i + 1)
                    wait(dve, pe_stage, step)
                    for t in range(2):
                        ins = dve.scalar_tensor_tensor(out=tq[i][:, t], in0=ps[:, (Q0, K0)[i]:(Q0, K0)[i] + 2, :],
                                                       scalar=winv[:, i:i + 1], in1=trig[:, t, :, c * CH:(c + 1) * CH],
                                                       op0=ALU.mult, op1=ALU.mult)
                    ins.then_inc(rot_mul.sem, 1)

                def third_part(step, i):
                    wait(dve, part2, step, i + 1)
                    dve.tensor_tensor(parts[i][step[1]][:, 2], r1[i][:, :, :], parts[i][step[1]][:, 1],
                                      ALU.subtract).then_inc(part3.sem, 1)

                def hidden(step, m):
                    before, mb = slot_user(step, m)
                    wait(dve, hid_hi, before, mb + 1)
                    wait_low(dve, before, mb)
                    wait(dve, silu, step, m + 1)
                    dve.scalar_tensor_tensor(out=h32[:, m % NH], in0=ps[:, FFN[m] + 1, :], scalar=QSCALE * HSCALE,
                                             in1=sg[:, m % NH], op0=ALU.mult, op1=ALU.mult).then_inc(hid.sem, 1)

                take_low((0, 0))

                def chunk(step, more):
                    rotate(step, 0, q_pe)
                    rotate(step, 1, k_pe)
                    if more:
                        stats(dve, nxt(step))
                    rest(dve, step, 0)
                    hidden(step, 0)
                    hidden(step, 1)
                    if more:
                        normalise(dve, nxt(step))
                    hidden(step, 2)
                    third_part(step, 0)
                    hidden(step, 3)
                    third_part(step, 1)
                    hidden(step, 4)
                    hidden(step, 5)
                    for m in range(LOW_POOL, MH):
                        low(dve, step, m)
                    if more:
                        take_low(nxt(step))

                over_batches(dve, chunk)

            @block.gpsimd
            def _(pool):
                for s in (rot_add, rest1[1], lo_pool):
                    s.start(pool)

                def rotated(step, i):
                    wait(pool, part1, earlier(step, 1), i + 1)
                    wait(pool, rest1[i], earlier(step, 1))
                    wait(pool, rot_mul, step, i + 1)
                    pool.tensor_tensor(rr[i][:, :, :], tq[i][:, :, 0, :], tq[i][:, :, 1, :], ALU.add).then_inc(rot_add.sem, 1)

                def chunk(step, more):
                    rotated(step, 0)
                    rotated(step, 1)
                    if more:
                        inverse_root(pool, nxt(step))
                    rest(pool, step, 1)
                    for m in range(LOW_POOL):
                        low(pool, step, m)
                        if m == 0 and more:
                            low_tokens(pool, nxt(step))

                over_batches(pool, chunk)

            @block.scalar
            def _(act):
                for s in (t_hi, part1, part2, v_act, silu, hid_hi, gate_act):
                    s.start(act)

                def take_high(step):
                    wait(act, t_pe, step)
                    act.activation(xTh.rearrange("p k s -> p (k s)")[:, :], ps[:, T0, :].bitcast(F16), ACT.Copy).then_inc(t_hi.sem, 1)

                def part(step, i, which):
                    dst, src = parts[i][step[1]], (rr, r1)[which][i]
                    if which == 0:
                        wait(act, qk_st, earlier(step, 2))
                        wait(act, rot_add, step, i + 1)
                    else:
                        wait(act, rest1[i], step)
                    act.activation(dst[:, which], src[:, :, :], ACT.Copy).then_inc((part1, part2)[which].sem, 1)

                def values(step):
                    wait(act, v_st, earlier(step, 1))
                    wait(act, v_pe, step)
                    act.activation(vs[:, :, :, 0:DK].rearrange("p a h v -> p (a h) v"),
                                   ps[:, V0:V0 + 2, :].rearrange("p c (h v) -> p (c h) v", v=DK),
                                   ACT.Copy).then_inc(v_act.sem, 1)

                def gate(step, m):
                    before, mb = slot_user(step, m)
                    wait(act, hid, before, mb + 1)
                    wait(act, gu_pe, step, m + 1)
                    act.activation(sg[:, m % NH], ps[:, FFN[m], :], ACT.Silu, scale=QSCALE).then_inc(silu.sem, 1)

                def high(step, m):
                    if m == 0:
                        wait(act, down_pe, earlier(step, 1))
                    wait(act, hid, step, m + 1)
                    act.activation(hh[:, m], h32[:, m % NH], ACT.Copy).then_inc(hid_hi.sem, 1)

                take_high((0, 0))

                def chunk(step, more):
                    if step[1] == 0:
                        act.activation(table[:, :], table[:, :], ACT.Silu).then_inc(s_held, 1)
                    part(step, 0, 0)
                    values(step)
                    gate(step, 0)
                    part(step, 1, 0)
                    gate(step, 1)
                    high(step, 0)
                    part(step, 0, 1)
                    gate(step, 2)
                    if more:
                        high_tokens(act, nxt(step))
                    gate(step, 3)
                    high(step, 1)
                    part(step, 1, 1)
                    high(step, 2)
                    for m in range(4, MH):
                        gate(step, m)
                        high(step, m - 1)
                    high(step, MH - 1)
                    if more:
                        take_high(nxt(step))
                    wait(act, g_st, earlier(step, 2))
                    for j in range(2):
                        wait(act, down_pe, step, j + 1)
                        act.activation(gs[:, step[1], 2 * j:2 * j + 2].rearrange("p a d -> p (a d)"), ps[:, V0 + j, :],
                                       ACT.Silu, scale=QSCALE / HSCALE).then_inc(gate_act.sem, 1)

                over_batches(act, chunk)

            @block.tensor
            def _(pe):
                for s in (q_pe, k_pe, v_pe, gu_pe, down_pe):
                    s.start(pe)

                def transposes(step):
                    wait(pe, t_lo, earlier(step, 1))
                    wait(pe, t_hi, earlier(step, 1))
                    wait(pe, x_lo, step)
                    for n, src in enumerate((xh, xl)):
                        for kd in range(KD):
                            for a in range(CT):
                                o = kd * CH + a * P
                                ins = pe.transpose(ps[:, T0 + n, :].bitcast(F16)[:, o:o + P], src[:, a, kd * P:(kd + 1) * P],
                                                   identh[:, :])
                    ins.then_inc(t_pe.sem, 1)

                transposes((0, 0))

                def chunk(step, more):
                    wait(pe, t_hi, step)
                    wait(pe, t_lo, step)
                    products = ((xTh, 0), (xTl, 0), (xTh, 1))
                    terms = [(kd, xx, wp) for kd in range(KD) for xx, wp in products]
                    for i, done in enumerate((q_pe, k_pe)):
                        wait(pe, hid, earlier(step, 1), (MH, MH - 1)[i])
                        for eo in range(2):
                            for n, (kd, xx, wp) in enumerate(terms):
                                ins = pe.matmul(ps[:, (Q0, K0)[i] + eo, :], wqkT[:, wp, kd, 2 * i + eo, :], xx[:, kd, :],
                                                start=n == 0, stop=n == len(terms) - 1)
                        ins.then_inc(done.sem, 1)
                    wait(pe, gate_act, earlier(step, 1))
                    for a in range(CT):
                        for n, (kd, xx, wp) in enumerate(terms):
                            ins = pe.matmul(ps[:, V0 + a // 2, (a % 2) * D:(a % 2 + 1) * D], xx[:, kd, a * P:(a + 1) * P],
                                            wvT[:, wp, kd, :], start=n == 0, stop=n == len(terms) - 1)
                    ins.then_inc(v_pe.sem, 1)
                    for m in range(MH):
                        if m < 2:
                            wait(pe, rot_mul, step, m + 1)
                        elif m == 2:
                            wait(pe, v_act, step)
                        else:
                            wait(pe, hid, step, {3: 1, 4: 2, 5: 4}[m])
                        for gu in range(2):
                            n = 0
                            for kd in range(KD):
                                for xx in (xTh, xTl):
                                    ins = pe.matmul(ps[:, FFN[m] + gu, :], wguT[:, gu, kd, m * P:(m + 1) * P],
                                                    xx[:, kd, :], start=n == 0, stop=n == 2 * KD - 1)
                                    n += 1
                        ins.then_inc(gu_pe.sem, 1)
                    if more:
                        transposes(nxt(step))
                    wait(pe, hid, step, 3)

                    def down(a, part, ms):
                        for m in ms:
                            if part is hh and a == 0:
                                wait(pe, hid_hi, step, m + 1)
                            if part is hl and a == 0:
                                wait_low(pe, step, m)
                            ins = pe.matmul(ps[:, V0 + a // 2, (a % 2) * D:(a % 2 + 1) * D], part[:, m, a * P:(a + 1) * P],
                                            wdT[:, m, :], start=part is hh and m == 0 and a % 2 == 0,
                                            stop=part is hl and m == MH - 1, skip_group_check=True)
                        return ins

                    for a in (0, 2):
                        down(a, hh, range(MH - 1))
                    for a in (0, 2):
                        down(a, hh, (MH - 1,))
                    for a in (1, 3):
                        down(a, hh, range(MH))
                    for a in range(CT):
                        ins = down(a, hl, range(MH))
                        if a % 2 == 1:
                            ins.then_inc(down_pe.sem, 1)

                over_batches(pe, chunk)



def score_units(by_key):
    units = []
    if by_key:
        for c in range(S // CH):
            for kb in range((c + 1) * CT):
                lo = max(kb * P, c * CH)
                w = (c + 1) * CH - lo
                n = min(GH, CH // w)
                units += [(kb, lo, w, tuple(range(h, h + n))) for h in range(0, GH, n)]
    else:
        for qb in range(QB):
            for lo in range(0, (qb + 1) * P, CH):
                w = min(CH, (qb + 1) * P - lo)
                n = 1 << ((CH // w).bit_length() - 1)
                n = min(GH, n)
                units += [(qb, lo, w, tuple(range(h, h + n))) for h in range(0, GH, n)]
    return units


def load_stacks(sp, keep, parts_d, step):
    b, g = step
    q_v, k_v = (d.rearrange("b (r h) s -> b r h s", h=H) for d in parts_d)
    h = slice(g * GH, (g + 1) * GH)
    qs, ks, ld = keep["qs"][g], keep["ks"][g], keep["qk_ld"][g]
    sp.dma_start(qs[0:3 * DK], q_v[b, 0:3 * DK, h]).then_inc(ld, 16)
    sp.dma_start(qs[3 * DK:5 * DK], q_v[b, 0:2 * DK, h]).then_inc(ld, 16)
    sp.dma_start(qs[5 * DK:6 * DK], q_v[b, 0:DK, h]).then_inc(ld, 16)
    for n, part in enumerate(K_BANDS):
        sp.dma_start(ks[n * DK:(n + 1) * DK], k_v[b, part * DK:(part + 1) * DK, h]).then_inc(ld, 16)


def attention_phase(nc, ps, keep, x, scratch, out):
    q_parts_d, k_parts_d, v_d, gate_d = scratch
    ident, woT = keep["ident"], keep["woT"]
    MAXU, EXPU = score_units(False), score_units(True)
    NU = len(MAXU)
    assert NU == len(EXPU)
    SHIFT = 13
    NSTEP = sum((c + 1) * CT for c in range(S // CH))
    diag_units = [u for u, (kb, lo, w, hs) in enumerate(EXPU) if lo == kb * P]
    ND = len(diag_units)
    ctx = ExitStack()
    with ctx:
        sb = lambda n, s, d: ctx.enter_context(nc.sbuf_tensor(n, s, d))
        sem = lambda n: ctx.enter_context(nc.semaphore(n))
        stage = lambda n, k: Stage(ctx, nc, n, k, NG)

        ROWS = STACK + PARTS
        for g in range(1, NG):
            keep["qs"].append(sb(f"qs{g}", [P, GH, S], BF16))
            keep["ks"].append(sb(f"ks{g}", [P, GH, S], BF16))
        qs, ks, qk_ld, g_st = keep["qs"], keep["ks"], keep["qk_ld"], keep["g_st"]
        vt = [sb(f"vt{i}", [P, QB, GH, VW], F32) for i in range(2)]
        pr = [sb(f"pr{i}", [P, GH, CH], F32) for i in range(3)]
        mxa = [sb(f"mxa{i}", [P, GH, QB], F32) for i in range(2)]
        mxb = [sb(f"mxb{i}", [P, GH, QB // 2], F32) for i in range(2)]
        mneg = sb("mneg", [GH * QB, P], F32)
        mp = sb("mp", [GH * QB, PARTS, P], BF16)
        mr = sb("mr", [GH * QB, P], F32)
        ot = sb("ot", [P, 2, CH], F32)
        rec = sb("rec", [P, 2, CT * GH], F32)
        an = sb("an", [P, QB, D], F32)
        ab = sb("ab", [P, QB, D], F32)
        gt = sb("gt", [P, HALVES, CT, D], F32)
        xt = sb("xt", [P, HALVES, CT, D], F32)
        zt = sb("zt", [P, HALVES, CT, D], F32)
        yt = sb("yt", [P, 2, D], F32)
        aT = sb("aT", [P, 2, KD, P], F32)
        table = sb("table", [1, 1], F32)
        identb = sb("identb", [P, P], BF16)
        future = sb("future", [P, P], BF16)

        s_c = sem("s_c")
        s_held = sem("s_held2")
        s_cl = sem("s_cl")
        v_ld = [sem(f"v_ld{g}") for g in range(2)]
        max_pe, max_dve = stage("max_pe", NU), stage("max_dve", NU)
        mx_join, mx_t, mx_neg, mx_parts = stage("mx_join", 1), stage("mx_t", 1), stage("mx_neg", 1), stage("mx_parts", 4)
        mx_ld = stage("mx_ld", 16 * PARTS)
        st_pe, expo, causal = stage("st_pe", NU), stage("expo", NU), stage("causal", ND)
        pv_pe, o_act, o_pe = stage("pv_pe", NSTEP), stage("o_act", 2), stage("o_pe", 2)
        o_rec, o_norm = stage("o_rec", 2), stage("o_norm", 2)
        s_copy = sem("s_copy")
        o_ld = [sem(f"o_ld{c}") for c in range(HALVES)]
        t_tr, t_ev, t_wo, t_mul, t_add = (Stage(ctx, nc, n, 1, QB) for n in ("t_tr", "t_ev", "t_wo", "t_mul", "t_add"))
        o_st = [Stage(ctx, nc, f"o_st{c}", 16, 1) for c in range(HALVES)]

        NST, NMX = 3, 3
        ST0, MX0, O0, M0 = 0, NST, NST + NMX, NST + NMX + 1
        LOADS = 16 * 9

        parts_d = q_parts_d, k_parts_d
        halves = lambda d: d.rearrange("b (c a p) d -> b c p a d", c=HALVES, p=P)
        x_v, gate_v, out_v = halves(x), halves(gate_d), halves(out)

        def nth(step, n):
            b, g = step
            d = (g + n) // NG
            return (b + d if d else b), (g + n) % NG

        def before_bank(units_k, step, u, nb):
            lst = [v for v in range(u) if v % nb == u % nb]
            if lst:
                return step, lst[-1] + 1
            lst = [v for v in range(units_k) if v % nb == u % nb]
            return earlier(step, 1), lst[-1] + 1

        with nc.Block() as block:

            def over_groups(eng, group):
                ahead_of = lambda g: lambda n: (B - 1) * NG + g + n < B * NG
                group((0, 0), False, lambda n: True)
                def batch(b):
                    for g in range(1, NG):
                        group((b, g), True, lambda n: True)
                    group((b + 1, 0), True, lambda n: True)
                batch(0)
                with eng.Fori(1, B - 1) as b:
                    batch(b)
                for g in range(1, NG):
                    group((B - 1, g), True, ahead_of(g))

            def output_tiles(step):
                b, g = step
                tiles = ((b - 2, QB - 1), (b - 1, 0)) if g == 0 else ((b - 1, 2 * g - 1), (b - 1, 2 * g))
                return [None if isinstance(t[0], int) and t[0] < 0 else t for t in tiles]

            last_tiles = [(B - 2, QB - 1)] + [(B - 1, t) for t in range(QB)]
            TILE_BANKS = NMX

            def maxima_of(step, ahead):
                out = []
                if ahead(1):
                    out += [(nth(step, 1), u) for u in range(SHIFT, NU)]
                if ahead(2):
                    out += [(nth(step, 2), u) for u in range(SHIFT)]
                return out

            first_maxima = [((0, 0), u) for u in range(NU)] + [((0, 1), u) for u in range(SHIFT)]

            def key_step(u):
                kb, lo, w, hs = EXPU[u]
                c = lo // CH
                return (CT if c else 0) + kb if c else kb

            LAG = 4
            last_of = {}
            for u in range(NU):
                last_of[key_step(u)] = u
            late = [s for s in range(NSTEP) if last_of[s] + LAG >= NU]
            TAKE1 = last_of[NSTEP - 1] + LAG - NU + 1
            OUT1 = TAKE1 + 4
            NORM1 = OUT1 + 2
            TAKE0 = last_of[CT - 1] + LAG + 1
            OUT0 = TAKE0 + 4
            NORM0 = OUT0 + 2
            MAXT = NU - SHIFT + 2
            NEG = MAXT + 1
            TR = (1, 30)
            WO = (4, 33)
            SPLIT_AT = [u for u in diag_units if u > NEG][0]

            def step_before(step, s, n):
                return (step, s - n + 1) if s >= n else (earlier(step, 1), NSTEP + s - n + 1)

            @block.sync
            def _(sp):
                mx_ld.start(sp)
                for s in o_st:
                    s.start(sp)
                def load_v(step):
                    b, g = step
                    sp.dma_start(vt[g % 2].rearrange("p k h v -> p k (h v)")[:, :, :],
                                 v_d.rearrange("b k p e -> b p k e")[b, :, :, g * GH * VW:(g + 1) * GH * VW]).then_inc(v_ld[g % 2], 16)

                def load_max(step):
                    g = step[1]
                    wait(sp, st_pe, earlier(step, NG))
                    for part in range(PARTS):
                        wait(sp, mx_parts, step, (1, 3, 4)[part])
                        sp.dma_start(qs[g][STACK + part:STACK + part + 1].rearrange("p h (q s) -> p (h q) s", q=QB),
                                     mp[:, part, :]).then_inc(mx_ld.sem, 16)

                for g in range(1, NG - 1):
                    load_stacks(sp, keep, parts_d, (0, g))
                for g in range(2):
                    load_v((0, g))
                load_max((0, 0))

                def copy_attention(b):
                    wait(sp, o_norm, (b, NG - 1))
                    wait(sp, t_tr, (b - 1, QB - 1))
                    sp.dma_start(ab[:, :, :], an[:, :, :]).then_inc(s_copy, 16)

                def load_output(b, c):
                    if isinstance(b, int) and b == 0 and c == 0:
                        wait(sp, g_st, (B - 1, HALVES - 1))
                    wait(sp, t_add, (b - 1, (c + 1) * CT - 1))
                    sp.dma_start(gt[:, c], gate_v[b, c]).then_inc(o_ld[c], 16)
                    sp.dma_start(xt[:, c], x_v[b, c]).then_inc(o_ld[c], 16)

                def store_output(b, c):
                    wait(sp, t_add, (b, (c + 1) * CT - 1))
                    sp.dma_start(out_v[b, c], zt[:, c]).then_inc(o_st[c].sem, 16)

                def group(step, prev, ahead):
                    b, g = step
                    if ahead(3):
                        wait(sp, st_pe, earlier(step, 1))
                        load_stacks(sp, keep, parts_d, nth(step, 3))
                    if prev:
                        if ahead(1):
                            wait(sp, pv_pe, nth(step, -1))
                            load_v(nth(step, 1))
                    before = output_tiles((b, 1))[0]
                    if g == 0 and prev:
                        copy_attention(b - 1)
                    if g == 1 and before:
                        load_output(b - 1, 1)
                    if g == NG - 1:
                        if before:
                            store_output(b - 1, 0)
                        load_output(b, 0)
                    if ahead(1):
                        load_max(nth(step, 1))
                    if g == 0 and output_tiles(step)[0]:
                        store_output(b - 2, 1)

                over_groups(sp, group)
                store_output(B - 2, 1)
                load_output(B - 1, 1)
                for c in range(HALVES):
                    store_output(B - 1, c)
                for c in range(HALVES):
                    wait(sp, o_st[c], (B - 1, 0))

            @block.gpsimd
            def _(pool):
                for s in (mx_parts, causal, t_add):
                    s.start(pool)
                ch = Chain(pool, s_c)
                ch(pool.memset(identb[:, :], 0.0))
                ch(pool.memset(future[:, :], 0.0))
                ch(pool.affine_select(out=identb[:, :], in_=identb[:, :], compare_op=ALU.not_equal, fill=1.0,
                                      base=0, pattern=[[-1, P]], channel_multiplier=1))
                ch(pool.affine_select(out=future[:, :], in_=future[:, :], compare_op=ALU.is_ge, fill=MASKED,
                                      base=0, pattern=[[-1, P]], channel_multiplier=1))

                ch(pool.memset(table[:, :], 0.0))

                for g in range(NG):
                    ins = pool.memset(ks[g][STACK:ROWS].bitcast(F32), ONES_TWICE)
                ins.then_inc(s_cl, 1)

                def split_max(step):
                    wait(pool, mx_ld, earlier(step, 1))
                    wait(pool, mx_neg, step)
                    hold(pool, s_held)
                    pool.tensor_scalar(mp[:, 0], mneg[:, :], 1.0, 0.0, ALU.mult, ALU.add).then_inc(mx_parts.sem, 1)
                    wait(pool, mx_parts, step, 1)
                    pool.tensor_tensor(mr[:, :], mneg[:, :], mp[:, 0], ALU.subtract).then_inc(mx_parts.sem, 1)
                    wait(pool, mx_parts, step, 2)
                    hold(pool, s_held)
                    pool.tensor_scalar(mp[:, 1], mr[:, :], 1.0, 0.0, ALU.mult, ALU.add).then_inc(mx_parts.sem, 1)
                    wait(pool, mx_parts, step, 3)
                    pool.tensor_tensor(mp[:, 2], mr[:, :], mp[:, 1], ALU.subtract).then_inc(mx_parts.sem, 1)

                def mask(step, n):
                    kb, lo, w, hs = EXPU[diag_units[n]]
                    s = key_step(diag_units[n])
                    blk = pr[s % 3][:, hs[0]:hs[-1] + 1, 0:P]
                    wait(pool, expo, step, diag_units[n] + 1)
                    hold(pool, s_held)
                    pool.affine_select(out=blk, in_=blk, compare_op=ALU.is_ge, fill=0.0, base=0,
                                       pattern=[[0, len(hs)], [1, P]], channel_multiplier=-1).then_inc(causal.sem, 1)

                def add_tile(tile):
                    b, t = tile
                    c = t // CT
                    wait(pool, o_st[c], (b - 1, 0))
                    wait(pool, t_mul, tile)
                    pool.tensor_tensor(zt[:, c, t % CT], yt[:, t % 2], xt[:, c, t % CT], ALU.add).then_inc(t_add.sem, 1)

                split_max((0, 0))

                def group(step, prev, ahead):
                    tiles = output_tiles(step)
                    for n in range(ND):
                        if diag_units[n] == SPLIT_AT and ahead(1):
                            split_max(nth(step, 1))
                        mask(step, n)
                        if diag_units[n] == last_of[CT - 1] and tiles[0]:
                            add_tile(tiles[0])
                    if tiles[1]:
                        add_tile(tiles[1])

                over_groups(pool, group)
                for tile in last_tiles:
                    add_tile(tile)

            def maximum(dve, step, u):
                qb, lo, w, hs = MAXU[u]
                par = step[1] % 2
                dst = mxa[par][:, hs[0]:hs[-1] + 1, qb] if lo == 0 else mxb[par][:, hs[0]:hs[-1] + 1, qb - QB // 2]
                if u == 0:
                    wait(dve, mx_t, earlier(step, 2))
                    wait(dve, mx_join, earlier(step, 2))
                wait(dve, max_pe, step, u + 1)
                dve.tensor_reduce(dst, ps[:, MX0 + u % NMX, 0:w * len(hs)].rearrange("p (h s) -> p h s", s=w),
                                  axis=AX.X, op=ALU.max).then_inc(max_dve.sem, 1)

            def join_max(dve, step):
                par = step[1] % 2
                wait(dve, max_dve, step)
                dve.tensor_tensor(mxa[par][:, :, QB // 2:], mxa[par][:, :, QB // 2:], mxb[par][:, :, :],
                                  ALU.max).then_inc(mx_join.sem, 1)

            def negate_max(dve, step):
                wait(dve, mx_parts, earlier(step, 1))
                wait(dve, mx_t, step)
                dve.tensor_scalar(mneg[:, :], ps[0:GH * QB, M0, 0:P], -1.0, None, ALU.mult).then_inc(mx_neg.sem, 1)

            @block.vector
            def _(dve):
                for s in (max_dve, mx_join, mx_neg, o_rec, o_norm, t_mul):
                    s.start(dve)
                def normalise(step, c):
                    o = ps[:, M0, :].rearrange("p (r v) -> p r v", v=VW)
                    b, g = step
                    if g == 0 and c == 0 and output_tiles((b, 1))[0]:
                        dve.wait_ge(s_copy, b * 16)
                    wait(dve, o_norm, earlier(step, 1), c + 1)
                    wait(dve, o_pe, step, c + 1)
                    dve.reciprocal(rec[:, c], o[:, :, DK]).then_inc(o_rec.sem, 1)
                    wait(dve, o_rec, step, c + 1)
                    dve.tensor_tensor(an[:, c * CT:(c + 1) * CT, g * GH * DK:(g + 1) * GH * DK].rearrange("p q (h e) -> p q h e", e=DK),
                                      o[:, :, 0:DK].rearrange("p (q h) e -> p q h e", h=GH),
                                      rec[:, c].rearrange("p (q h) -> p q h", h=GH).unsqueeze(3).to_broadcast([P, CT, GH, DK]),
                                      ALU.mult).then_inc(o_norm.sem, 1)

                def gate_tile(tile, bank):
                    b, t = tile
                    c = t // CT
                    if t % CT == 0:
                        dve.wait_ge(o_ld[c], b * 32 + 32)
                    wait(dve, t_add, earlier(tile, 2))
                    wait(dve, t_wo, tile)
                    dve.tensor_tensor(yt[:, t % 2], ps[:, bank, D:2 * D], gt[:, c, t % CT], ALU.mult).then_inc(t_mul.sem, 1)

                for ms, u in first_maxima:
                    maximum(dve, ms, u)
                    if (ms, u) == ((0, 0), NU - 1):
                        join_max(dve, ms)
                        negate_max(dve, ms)

                def group(step, prev, ahead):
                    todo = maxima_of(step, ahead)
                    tiles = output_tiles(step)
                    for n in range(NU):
                        if n < len(todo):
                            ms, u = todo[n]
                            maximum(dve, ms, u)
                            if u == NU - 1:
                                join_max(dve, ms)
                        if n == NORM1 and prev:
                            normalise(nth(step, -1), 1)
                        if n == NORM0:
                            normalise(step, 0)
                        if n == NEG and ahead(1):
                            negate_max(dve, nth(step, 1))
                        for i in range(2):
                            if n == WO[i] + 1 and tiles[i]:
                                gate_tile(tiles[i], M0)

                over_groups(dve, group)
                normalise((B - 1, NG - 1), 1)
                for i, tile in enumerate(last_tiles):
                    gate_tile(tile, MX0 + i % TILE_BANKS)

            @block.scalar
            def _(act):
                for s in (expo, o_act, t_ev):
                    s.start(act)

                act.wait_ge(s_c, 5)
                act.activation(table[:, :], table[:, :], ACT.Exp).then_inc(s_held, 1)

                def exponentials(step, u):
                    kb, lo, w, hs = EXPU[u]
                    s = key_step(u)
                    prev = step_before(step, s, 3)
                    wait(act, pv_pe, *prev)
                    wait(act, st_pe, step, u + 1)
                    act.activation(pr[s % 3][:, hs[0]:hs[-1] + 1, 0:w],
                                   ps[:, ST0 + u % NST, 0:w * len(hs)].rearrange("p (h s) -> p h s", s=w),
                                   ACT.Exp, scale=1.0 / DK ** 0.5).then_inc(expo.sem, 1)

                def take_output(step, c):
                    wait(act, o_pe, earlier(step, 1), c + 1)
                    wait(act, pv_pe, step, CT if c == 0 else NSTEP)
                    act.activation(ot[:, c], ps[:, O0, :], ACT.Copy).then_inc(o_act.sem, 1)

                def take_tile(tile, bank):
                    wait(act, t_wo, earlier(tile, 2))
                    wait(act, t_tr, tile)
                    act.activation(aT[:, tile[1] % 2], ps[:, bank, 0:D].rearrange("p (k t) -> p k t", k=KD),
                                   ACT.Copy).then_inc(t_ev.sem, 1)

                def group(step, prev, ahead):
                    tiles = output_tiles(step)
                    for u in range(NU):
                        exponentials(step, u)
                        for i in range(2):
                            if u == TR[i] + 1 and tiles[i]:
                                take_tile(tiles[i], M0)
                        if u == TAKE1 and prev:
                            take_output(nth(step, -1), 1)
                        if u == TAKE0:
                            take_output(step, 0)

                over_groups(act, group)
                take_output((B - 1, NG - 1), 1)
                for i, tile in enumerate(last_tiles):
                    take_tile(tile, MX0 + i % TILE_BANKS)

            @block.tensor
            def _(pe):
                for s in (max_pe, mx_t, st_pe, pv_pe, o_pe, t_tr, t_wo):
                    s.start(pe)
                pe.wait_ge(s_c, 4)

                def queries_by_keys(step, u):
                    qb, lo, w, hs = MAXU[u]
                    b, g = step
                    if u == 0:
                        pe.wait_ge(qk_ld[g], b * LOADS + LOADS)
                    wait(pe, max_dve, *before_bank(NU, step, u, NMX))
                    diag = lo + w > qb * P
                    for n, h in enumerate(hs):
                        o = ps[:, MX0 + u % NMX, n * w:(n + 1) * w]
                        ins = pe.matmul(o, qs[g][0:STACK, h, qb * P:(qb + 1) * P], ks[g][0:STACK, h, lo:lo + w],
                                        start=n == 0, stop=not diag, skip_group_check=True)
                        if diag:
                            ins = pe.matmul(o[:, w - P:w], identb[:, :], future[:, :], start=False, stop=True,
                                            skip_group_check=True)
                    ins.then_inc(max_pe.sem, 1)

                def keys_by_queries(step, u):
                    kb, lo, w, hs = EXPU[u]
                    g = step[1]
                    if u == 0:
                        wait(pe, mx_ld, step)
                    wait(pe, expo, *before_bank(NU, step, u, NST))
                    for n, h in enumerate(hs):
                        ins = pe.matmul(ps[:, ST0 + u % NST, n * w:(n + 1) * w], ks[g][0:ROWS, h, kb * P:(kb + 1) * P],
                                        qs[g][0:ROWS, h, lo:lo + w], start=True, stop=True)
                    ins.then_inc(st_pe.sem, 1)

                def times_v(step, s):
                    b, g = step
                    c = 0 if s < CT else 1
                    kb = s if s < CT else s - CT
                    lo = max(kb * P - c * CH, 0)
                    if s == 0:
                        pe.wait_ge(v_ld[g % 2], b * 32 + 16 * (g // 2) + 16)
                    if kb == 0:
                        wait(pe, o_act, *((step, 1) if c else (earlier(step, 1), 2)))
                    nd = [n for n, u in enumerate(diag_units) if key_step(u) == s]
                    if nd:
                        wait(pe, causal, step, nd[-1] + 1)
                    wait(pe, expo, step, last_of[s] + 1)
                    for j in range(GH):
                        ins = pe.matmul(ps[VW * j:VW * (j + 1), O0, lo:CH], vt[g % 2][:, kb, j, :],
                                        pr[s % 3][:, j, 0:CH - lo], start=kb == 0, stop=kb == (c + 1) * CT - 1)
                    ins.then_inc(pv_pe.sem, 1)

                def transpose_max(step):
                    wait(pe, o_norm, earlier(step, 1), 1)
                    wait(pe, mx_join, step)
                    pe.matmul(ps[0:GH * QB, M0, 0:P], mxa[step[1] % 2].rearrange("p h q -> p (h q)")[:, :], ident[:, :],
                              start=True, stop=True).then_inc(mx_t.sem, 1)

                def transpose_output(step, c, tile=None):
                    if c == 0:
                        wait(pe, o_norm, earlier(step, 1))
                    elif tile:
                        wait(pe, t_mul, tile)
                    else:
                        wait(pe, mx_neg, nth(step, 1))
                    wait(pe, o_norm, step, c)
                    wait(pe, o_act, step, c + 1)
                    for a in range(CT):
                        ins = pe.transpose(ps[:, M0, a * P:(a + 1) * P], ot[:, c, a * P:(a + 1) * P], ident[:, :])
                    ins.then_inc(o_pe.sem, 1)

                def transpose_tile(tile, bank, source):
                    t = tile[1]
                    for kd in range(KD):
                        ins = pe.transpose(ps[:, bank, kd * P:(kd + 1) * P], source[:, t, kd * P:(kd + 1) * P], ident[:, :])
                    ins.then_inc(t_tr.sem, 1)

                def project_tile(tile, bank):
                    wait(pe, t_ev, tile)
                    for kd in range(KD):
                        ins = pe.matmul(ps[:, bank, D:2 * D], aT[:, tile[1] % 2, kd, :], woT[:, kd, :],
                                        start=kd == 0, stop=kd == KD - 1)
                    ins.then_inc(t_wo.sem, 1)

                for ms, u in first_maxima:
                    queries_by_keys(ms, u)
                    if (ms, u) == ((0, 0), NU - 1):
                        transpose_max((0, 0))
                pe.wait_ge(s_cl, 1)

                def group(step, prev, ahead):
                    todo = maxima_of(step, ahead)
                    tiles = output_tiles(step)
                    for n in range(NU):
                        keys_by_queries(step, n)
                        if n < len(todo):
                            queries_by_keys(*todo[n])
                        for s in range(NSTEP):
                            if last_of[s] + LAG == n:
                                times_v(step, s)
                            if prev and last_of[s] + LAG == n + NU:
                                times_v(nth(step, -1), s)
                        if n == TR[0] and tiles[0]:
                            wait(pe, t_mul, earlier(tiles[0], 1))
                            transpose_tile(tiles[0], M0, ab)
                        if n == TR[1] and tiles[1]:
                            if ahead(1):
                                wait(pe, mx_neg, nth(step, 1))
                            else:
                                wait(pe, o_norm, step, 1)
                            if tiles[1][1] == 0:
                                pe.wait_ge(s_copy, (tiles[1][0] + 1) * 16)
                            transpose_tile(tiles[1], M0, ab)
                        for i in range(2):
                            if n == WO[i] and tiles[i]:
                                project_tile(tiles[i], M0)
                        if n == OUT1 and prev:
                            transpose_output(nth(step, -1), 1, tiles[0])
                        if n == OUT0:
                            transpose_output(step, 0)
                        if n == MAXT and ahead(1):
                            transpose_max(nth(step, 1))

                over_groups(pe, group)
                for s in late:
                    times_v((B - 1, NG - 1), s)

                def next_tile(i):
                    b, t = last_tiles[i]
                    bank = MX0 + i % TILE_BANKS
                    if i >= TILE_BANKS:
                        wait(pe, t_mul, last_tiles[i - TILE_BANKS])
                    if b == B - 1:
                        wait(pe, o_norm, (B - 1, NG - 1), t // CT + 1)
                    transpose_tile((b, t), bank, ab if b < B - 1 else an)

                wait(pe, max_dve, (B - 1, NG - 1))
                next_tile(0)
                transpose_output((B - 1, NG - 1), 1, output_tiles((B - 1, NG - 1))[1])
                for i in range(len(last_tiles)):
                    if i + 1 < len(last_tiles):
                        next_tile(i + 1)
                    project_tile(last_tiles[i], MX0 + i % TILE_BANKS)


def program(nc, x, wq, wk, wv, wo, w_gate, w_up, w_down, cs, out):
    nc.disable_value_cache = True
    q_parts_d = nc.dram_tensor("q_parts_d", [B, PARTS * 2 * P, S], BF16).ap()
    k_parts_d = nc.dram_tensor("k_parts_d", [B, PARTS * 2 * P, S], BF16).ap()
    v_d = nc.dram_tensor("v_d", [B, QB, P, H * VW], F32).ap()
    gate_d = nc.dram_tensor("gate_d", [B, S, D], F32).ap()
    with ExitStack() as ctx:
        ps = ctx.enter_context(nc.psum_tensor("ps", [P, 8, 512], F32))
        keep = {"ident": ctx.enter_context(nc.sbuf_tensor("ident", [P, P], F32)),
                "woT": ctx.enter_context(nc.sbuf_tensor("woT", [P, KD, D], F32)),
                "gs": ctx.enter_context(nc.sbuf_tensor("gs", [P, HALVES, CT, D], F32)),
                "qs": [ctx.enter_context(nc.sbuf_tensor("qs0", [P, GH, S], BF16))],
                "ks": [ctx.enter_context(nc.sbuf_tensor("ks0", [P, GH, S], BF16))],
                "qk_ld": [ctx.enter_context(nc.semaphore(f"qk_ld{g}")) for g in range(NG)],
                "g_st": Stage(ctx, nc, "g_st", 16, HALVES)}
        project_phase(nc, ps, keep, x, wq, wk, wv, wo, w_gate, w_up, w_down, cs, (q_parts_d, k_parts_d, v_d, gate_d))
        attention_phase(nc, ps, keep, x, (q_parts_d, k_parts_d, v_d, gate_d), out)


_INS = ["L0_attn_x", "L0_attn_wq", "L0_attn_wk", "L0_attn_wv", "L0_attn_wo", "L0_ffn_w_gate", "L0_ffn_w_up", "L0_ffn_w_down"]


def kernel(**inputs):
    import numpy as _np
    import concourse.bacc as _bacc
    from concourse import mybir as _mybir
    from concourse.bass_utils import run_bass_kernel_spmd as _run

    nc = _bacc.Bacc("TRN2", target_bir_lowering=False, num_devices=1)
    arrays, args = {}, []
    for name in _INS:
        a = _np.ascontiguousarray(inputs[name])
        arrays[f"in_{name}"] = a
        args.append(nc.dram_tensor(f"in_{name}", a.shape, _mybir.dt.from_np(a.dtype), kind="ExternalInput").ap())
    f = _np.float32
    angle = _np.arange(S, dtype=f)[:, None] / f(10000.0) ** (f(2.0) * _np.arange(PAIRS, dtype=f)[None, :] / f(DK))
    sin, cos = (_np.repeat(t(angle).T, H, axis=0) for t in (_np.sin, _np.cos))
    a = _np.ascontiguousarray(_np.stack([_np.stack([cos, -sin], 1), _np.stack([sin, cos], 1)], 1))
    arrays["in_trig"] = a
    args.append(nc.dram_tensor("in_trig", a.shape, F32, kind="ExternalInput").ap())
    args.append(nc.dram_tensor("out_dram", (B, S, D), F32, kind="ExternalOutput").ap())
    program(nc, *args)
    r = _run(nc, [arrays], core_ids=[0])
    return r.results[0]["out_dram"]
```
